# Optimizing a Trainium2 kernel written in Bass

```python
import numpy as np
import jax
import jax.numpy as jnp

def _softmax(x, axis=-1):
    return jax.nn.softmax(x, axis=axis)

def _gelu(x):
    return jax.nn.gelu(x, approximate=True)

def _silu(x):
    return jax.nn.silu(x)

def _sigmoid(x):
    return jax.nn.sigmoid(x)

def _layernorm(x, axis=-1, eps=1e-05):
    m = jnp.mean(x, axis=axis, keepdims=True)
    v = jnp.var(x, axis=axis, keepdims=True)
    return (x - m) / jnp.sqrt(v + eps)

def _scatter_add(tgt, idx, src, axis=0):
    return tgt.at[idx].add(src)

def _segment_sum(src, seg, n):
    return jax.ops.segment_sum(src, seg, n)
kernel_name = 'mk_seq_postln_d1_jaxref_r2_6e38d6'

def setup_inputs(seed: int=0):
    np.random.seed(seed)
    _w = jnp.asarray

    def _L0_attn_setup():
        import jax, jax.numpy as jnp
        import numpy as np

        def silu(x):
            return x * jax.nn.sigmoid(x)
        key = jax.random.key(seed)
        ks = jax.random.split(key, 9)
        d_model, d_inner, d_state, d_conv, dt_rank = (512, 1024, 16, 4, 64)
        B, L = (2, 512)
        s = 0.02
        return {'hidden_states': jax.random.normal(ks[0], (B, L, d_model), jnp.float32), 'in_proj_w': jax.random.normal(ks[1], (2 * d_inner, d_model), jnp.float32) * s, 'conv_w': jax.random.normal(ks[2], (d_inner, 1, d_conv), jnp.float32) * 0.2, 'conv_b': jax.random.normal(ks[3], (d_inner,), jnp.float32) * 0.1, 'x_proj_w': jax.random.normal(ks[4], (dt_rank + 2 * d_state, d_inner), jnp.float32) * s, 'dt_proj_w': jax.random.normal(ks[5], (d_inner, dt_rank), jnp.float32) * dt_rank ** (-0.5), 'dt_proj_b': jax.random.normal(ks[6], (d_inner,), jnp.float32) - 4.0, 'A_log': jnp.log(jnp.tile(jnp.arange(1.0, d_state + 1.0, dtype=jnp.float32)[None, :], (d_inner, 1))), 'D': jnp.ones((d_inner,), jnp.float32), 'out_proj_w': jax.random.normal(ks[7], (d_model, d_inner), jnp.float32) * s}
    _L0_attn_in = _L0_attn_setup()

    def _L0_ffn_setup():
        import jax, jax.numpy as jnp
        import numpy as np
        EPS = 1e-05

        def _quantize(W):
            gamma = jnp.mean(jnp.abs(W))
            return jnp.clip(jnp.round(W / (gamma + EPS)), -1.0, 1.0)
        key = jax.random.key(seed)
        k_x, k_w1, k_b1, k_w2, k_b2 = jax.random.split(key, 5)
        n_embd = 512
        d_ff = 4 * n_embd
        B, S = (4, 2048)
        bound1 = 1.0 / np.sqrt(n_embd)
        bound2 = 1.0 / np.sqrt(d_ff)
        x = jax.random.normal(k_x, (B, S, n_embd), dtype=jnp.float32)
        W1 = jax.random.uniform(k_w1, (d_ff, n_embd), jnp.float32, -bound1, bound1)
        b1 = jax.random.uniform(k_b1, (d_ff,), jnp.float32, -bound1, bound1)
        W2 = jax.random.uniform(k_w2, (n_embd, d_ff), jnp.float32, -bound2, bound2)
        b2 = jax.random.uniform(k_b2, (n_embd,), jnp.float32, -bound2, bound2)
        return {'x': x, 'W1': W1, 'b1': b1, 'W2': W2, 'b2': b2}
    _L0_ffn_in = _L0_ffn_setup()
    _d = {'L0_attn_hidden_states': _L0_attn_in['hidden_states'], 'L0_attn_in_proj_w': _L0_attn_in['in_proj_w'], 'L0_attn_conv_w': _L0_attn_in['conv_w'], 'L0_attn_conv_b': _L0_attn_in['conv_b'], 'L0_attn_x_proj_w': _L0_attn_in['x_proj_w'], 'L0_attn_dt_proj_w': _L0_attn_in['dt_proj_w'], 'L0_attn_dt_proj_b': _L0_attn_in['dt_proj_b'], 'L0_attn_A_log': _L0_attn_in['A_log'], 'L0_attn_D': _L0_attn_in['D'], 'L0_attn_out_proj_w': _L0_attn_in['out_proj_w'], 'L0_ffn_W1': _L0_ffn_in['W1'], 'L0_ffn_b1': _L0_ffn_in['b1'], 'L0_ffn_W2': _L0_ffn_in['W2'], 'L0_ffn_b2': _L0_ffn_in['b2']}
    _x0 = _d['L0_attn_hidden_states']
    _d['L0_attn_hidden_states'] = jax.random.normal(jax.random.fold_in(jax.random.key(seed), 1), (2, 4096, 512), dtype=_x0.dtype)
    del _x0
    return _d

def reference(L0_attn_hidden_states, L0_attn_in_proj_w, L0_attn_conv_w, L0_attn_conv_b, L0_attn_x_proj_w, L0_attn_dt_proj_w, L0_attn_dt_proj_b, L0_attn_A_log, L0_attn_D, L0_attn_out_proj_w, L0_ffn_W1, L0_ffn_b1, L0_ffn_W2, L0_ffn_b2):

    def _L0_attn_ref(hidden_states, in_proj_w, conv_w, conv_b, x_proj_w, dt_proj_w, dt_proj_b, A_log, D, out_proj_w):
        import jax, jax.numpy as jnp
        import numpy as np

        def silu(x):
            return x * jax.nn.sigmoid(x)
        Bsz, L, _ = hidden_states.shape
        d_inner, d_state = A_log.shape
        dt_rank = dt_proj_w.shape[1]
        K = conv_w.shape[-1]
        xz = jnp.einsum('bld,ed->ble', hidden_states, in_proj_w)
        x, z = (xz[..., :d_inner], xz[..., d_inner:])
        xp = jnp.pad(x, ((0, 0), (K - 1, 0), (0, 0)))
        w = conv_w[:, 0, :]
        x = sum((xp[:, k:k + L, :] * w[:, k] for k in range(K))) + conv_b
        x = silu(x)
        x_dbl = jnp.einsum('bld,ed->ble', x, x_proj_w)
        dt = x_dbl[..., :dt_rank]
        Bm = x_dbl[..., dt_rank:dt_rank + d_state]
        Cm = x_dbl[..., dt_rank + d_state:]
        dt = jax.nn.softplus(jnp.einsum('blr,dr->bld', dt, dt_proj_w) + dt_proj_b)
        A = -jnp.exp(A_log)
        deltaA = jnp.exp(jnp.einsum('bld,dn->bldn', dt, A))
        deltaB_u = jnp.einsum('bld,bln,bld->bldn', dt, Bm, x)

        def step(h, inp):
            dA_t, dBu_t, c_t = inp
            h = dA_t * h + dBu_t
            y_t = jnp.einsum('bdn,bn->bd', h, c_t)
            return (h, y_t)
        h0 = jnp.zeros((Bsz, d_inner, d_state), deltaA.dtype)
        _, ys = jax.lax.scan(step, h0, (deltaA.transpose(1, 0, 2, 3), deltaB_u.transpose(1, 0, 2, 3), Cm.transpose(1, 0, 2)))
        y = ys.transpose(1, 0, 2) + x * D
        y = y * silu(z)
        return jnp.einsum('bld,ed->ble', y, out_proj_w)

    def _L0_ffn_ref(x, W1, b1, W2, b2):
        import jax, jax.numpy as jnp
        import numpy as np
        EPS = 1e-05

        def _quantize(W):
            gamma = jnp.mean(jnp.abs(W))
            return jnp.clip(jnp.round(W / (gamma + EPS)), -1.0, 1.0)
        Wq1 = _quantize(W1)
        Wq2 = _quantize(W2)
        h = jax.nn.relu(jnp.einsum('bsd,fd->bsf', x, Wq1) + b1)
        out = jnp.einsum('bsf,df->bsd', h, Wq2) + b2
        return out
    x = L0_attn_hidden_states
    x = _layernorm(x + _L0_attn_ref(x, L0_attn_in_proj_w, L0_attn_conv_w, L0_attn_conv_b, L0_attn_x_proj_w, L0_attn_dt_proj_w, L0_attn_dt_proj_b, L0_attn_A_log, L0_attn_D, L0_attn_out_proj_w), axis=-1)
    x = _layernorm(x + _L0_ffn_ref(x, L0_ffn_W1, L0_ffn_b1, L0_ffn_W2, L0_ffn_b2), axis=-1)
    return x

_drawn_inputs = setup_inputs


def setup_inputs(seed=0):
    import zlib

    import numpy as np

    out = dict(_drawn_inputs(seed))
    spreads = {'L0_attn_D': (1.0, 0.6)}
    factors = {'L0_attn_in_proj_w': 3.363,
     'L0_attn_conv_w': 3.618,
     'L0_attn_conv_b': 7.094,
     'L0_attn_x_proj_w': 8.0,
     'L0_attn_dt_proj_w': 8.0,
     'L0_attn_dt_proj_b': 8.0,
     'L0_attn_A_log': 8.0,
     'L0_attn_out_proj_w': 3.197,
     'L0_ffn_b1': 41.943,
     'L0_ffn_b2': 64.0}
    for name, (base, spread) in spreads.items():
        noise = np.random.default_rng([zlib.crc32(name.encode()), seed]).standard_normal(out[name].shape)
        drawn = base * np.exp(spread * noise) if base else spread * noise
        out[name] = jnp.asarray(drawn.astype(out[name].dtype))
    for name, factor in factors.items():
        out[name] = (out[name] * factor).astype(out[name].dtype)
    return out
```

```python
from contextlib import ExitStack

import concourse.bass as bass
from concourse import mybir

F32 = mybir.dt.float32
F32R = mybir.dt.float32r
ALU = mybir.AluOpType
ACT = mybir.ActivationFunctionType
AX = mybir.AxisListType

P = 128
BATCH, SEQ, DM = 2, 4096, 512
DI, NS, KC, DTR = 1024, 16, 4, 64
DFF = 2048
TC = 512
CHUNKS = BATCH * SEQ // TC
CPB = SEQ // TC
NB = DI // P
KM = DM // P
TB = TC // P
HB = NB // 2
XD = DTR + 2 * NS
NJ = DFF // P
EPS_LN = 1e-5
EPS_Q = 1e-5
ONE_UP = 1.0 + 2.0 ** -23

STEPS = 2 * NS


class Tile:

    def __init__(self, index, bank, use, banks):
        self.index, self.bank, self.use, self.banks = index, bank, use, banks

    def full(self, it, per_chunk):
        return it * per_chunk + self.index + 1

    def empty(self, it):
        return it * self.banks[self.bank] + self.use + 1

    def read(self, it):
        return it * self.banks[self.bank] + self.use + 2


def gemm_tiles():
    order = [("x", i) for i in range(NB)] + [("z", i) for i in range(NB)]
    order += [("xdbl", 0), ("ct", 0)] + [("dt", i) for i in range(NB)]
    order += [("y", i) for i in range(NB)] + [("o", i) for i in range(TB)]
    uses, tiles = [0] * 4, {}
    for n, name in enumerate(order):
        bank = n % 4
        tiles[name] = Tile(n, bank, uses[bank], uses)
        uses[bank] += 1
    return tiles


def mixer_phase(nc, x_tm, x_cm, w_in, conv_w, conv_b, w_xp, w_dt, b_dt, a_log, d_skip, w_out, b_rows, x1):
    tiles = gemm_tiles()
    NG = len(tiles)
    ctx = ExitStack()
    with ctx:
        def sb(name, shape, dt=F32):
            return ctx.enter_context(nc.sbuf_tensor(name, shape, dt))

        def sem(name):
            return ctx.enter_context(nc.semaphore(name))

        win = sb("win", [P, KM, 2 * DI])
        wout = sb("wout", [P, NB, DM])
        wxp = sb("wxp", [P, NB, XD])
        wdt = sb("wdt", [DTR, DI])
        ident = sb("ident", [P, P])
        cw = sb("cw", [P, NB, KC])
        cb = sb("cb", [P, NB])
        bdt = sb("bdt", [P, NB])
        dsk = sb("dsk", [P, NB])
        aneg = sb("aneg", [P, NB, NS])
        minus1 = sb("minus1", [P, 1])
        epsln = sb("epsln", [P, 1])
        xt = sb("xt", [P, KM, TC])
        xres = sb("xres", [P, TB, DM])
        xpad = sb("xpad", [P, NB, KC - 1 + TC])
        x = sb("x", [P, NB, TC])
        z = sb("z", [P, NB, TC])
        dt = sb("dt", [P, NB, TC])
        dtx = sb("dtx", [P, NB, TC])
        yt = sb("yt", [P, TB, DI])
        bb = sb("bb", [P, 2, 2, TC])
        dbu = sb("dbu", [P, 2, 2, TC])
        h = sb("h", [P, 2, HB, TC])
        carry = sb("carry", [P, NS, NB])
        xdbl = sb("xdbl", [XD, TC])
        ct = sb("ct", [P, TB, XD])
        stats = sb("stats", [P, TB, 6])
        mv = sb("mv", [P, TB, 2])
        lnv = sb("lnv", [P, TB])
        rstd = sb("rstd", [P, TB])
        t2 = yt[:, :, :].rearrange("p a b -> p (a b)").rearrange("p (h n) -> p h n", h=2)
        t3 = h[:, :, :, :].rearrange("p s b t -> p s (b t)")
        dt_h = dt[:, :, :].rearrange("p (h b) t -> p h (b t)", h=2)
        dtx_h = dtx[:, :, :].rearrange("p (h b) t -> p h (b t)", h=2)
        x_h = x[:, :, :].rearrange("p (h b) t -> p h (b t)", h=2)

        G = [ctx.enter_context(nc.psum_tensor(f"gemm{i}", [P, 512], F32)) for i in range(4)]
        DA = [ctx.enter_context(nc.psum_tensor(f"decay{i}", [P, TC], F32)) for i in range(2)]
        HT = [ctx.enter_context(nc.psum_tensor(f"ht{i}", [P, 512], F32)) for i in range(2)]

        weights_in = sem("weights_in")
        alog_in = sem("alog_in")
        xt_in = sem("xt_in")
        x_in = sem("x_in")
        b_out = sem("b_out")
        bb_in = [sem("bb_in0"), sem("bb_in1")]
        x1_out = sem("x1_out")
        x1_seen = sem("x1_seen")
        consts_set = sem("consts_set")
        ident_zero = sem("ident_zero")
        ident_set = sem("ident_set")
        a_exp = sem("a_exp")
        a_set = sem("a_set")
        g_full = sem("g_full")
        g_free = [sem(f"g_free{i}") for i in range(4)]
        hist_zero = sem("hist_zero")
        hist_saved = sem("hist_saved")
        conv_step = sem("conv_step")
        x_ready = sem("x_ready")
        e_ready = sem("e_ready")
        u_ready = sem("u_ready")
        l1_ready = sem("l1_ready")
        l23_ready = sem("l23_ready")
        s1_ready = sem("s1_ready")
        s_ready = sem("s_ready")
        log1p_ready = sem("log1p_ready")
        dt_ready = sem("dt_ready")
        dtx_ready = sem("dtx_ready")
        decay_ready = sem("decay_ready")
        dbu_ready = sem("dbu_ready")
        scanned = sem("scanned")
        carried = sem("carried")
        ht_full = sem("ht_full")
        y_added = sem("y_added")
        gated = sem("gated")
        stats_ready = sem("stats_ready")
        stats_seen = sem("stats_seen")
        mv_ready = sem("mv_ready")
        lnv_ready = sem("lnv_ready")
        rstd_ready = sem("rstd_ready")
        x1_ready = sem("x1_ready")

        N_WEIGHTS = 8

        block = ctx.enter_context(nc.Block())

        @block.sync
        def _(sp):
            def load_xt(first):
                sp.dma_start(xt[:, :, :], x_cm.rearrange("(k p) t -> p k t", p=P)[:, :, bass.ds(first, TC)])\
                    .then_inc(xt_in, 16)

            load_xt(0)
            sp.dma_start(win[:, :, :], w_in.rearrange("(k p) e -> p k e", p=P)).then_inc(weights_in, 16)
            sp.dma_start(cw[:, :, :], conv_w).then_inc(weights_in, 16)
            for dst, src in ((cb, conv_b), (bdt, b_dt), (dsk, d_skip)):
                sp.dma_start(dst[:, :], src).then_inc(weights_in, 16)
            sp.dma_start(aneg[:, :, :], a_log).then_inc(alog_in, 16)
            sp.dma_start(wxp[:, :, :], w_xp.rearrange("(i p) e -> p i e", p=P)).then_inc(weights_in, 16)
            sp.dma_start(wdt[:, :], w_dt).then_inc(weights_in, 16)
            sp.dma_start(wout[:, :, :], w_out.rearrange("(i p) e -> p i e", p=P)).then_inc(weights_in, 16)

            def chunk(it, last):
                first = it * TC if last else sp.snap(it * TC)
                following = None if last else sp.snap(it * TC + TC)
                sp.dma_start(xres[:, :, :], x_tm[bass.ds(first, TC), :].rearrange("(a p) e -> p a e", p=P))\
                    .then_inc(x_in, 16)
                sp.wait_ge(g_free[tiles["xdbl", 0].bank], tiles["xdbl", 0].read(it))
                sp.dma_start(b_rows, xdbl[DTR:DTR + NS, :]).then_inc(b_out, 16)
                sp.wait_ge(b_out, it * 16 + 16)
                for pair in range(NS // 2):
                    slot = pair % 2
                    if pair >= 2:
                        sp.wait_ge(dbu_ready, it * (NS * HB) + (pair - 1) * 2 * HB)
                    sp.dma_start(bb[:, slot, :, :],
                                 b_rows[2 * pair:2 * pair + 2, :].rearrange("(o n) t -> o n t", o=1)
                                 .to_broadcast([P, 2, TC])).then_inc(bb_in[slot], 16)
                    if pair == 1 and not last:
                        sp.wait_ge(g_full, tiles["z", NB - 1].full(it, NG))
                        load_xt(following)
                sp.wait_ge(x1_ready, it + 1)
                sp.dma_start(x1[bass.ds(first, TC), :].rearrange("(a p) e -> p a e", p=P), xres[:, :, :])\
                    .then_inc(x1_out, 16)
                sp.wait_ge(x1_out, it * 16 + 16)
                sp.sem_inc(x1_seen, 1)

            with sp.Fori(0, CHUNKS - 1) as it:
                chunk(it, False)
            chunk(CHUNKS - 1, True)

        @block.gpsimd
        def _(pool):
            nc.gpsimd.memset(minus1[:, :], -1.0).then_inc(consts_set, 1)
            nc.gpsimd.memset(epsln[:, :], EPS_LN).then_inc(consts_set, 1)
            nc.gpsimd.memset(ident[:, :], 0.0).then_inc(ident_zero, 1)
            pool.wait_ge(ident_zero, 1)
            nc.gpsimd.affine_select(out=ident[:, :], in_=ident[:, :], compare_op=ALU.not_equal, fill=1.0,
                                    base=0, pattern=[[-1, P]], channel_multiplier=1).then_inc(ident_set, 1)
            for s in g_free + [hist_saved]:
                pool.sem_inc(s, 1)

            with pool.Fori(0, CHUNKS) as it:
                for hf in range(2):
                    pool.wait_ge(dt_ready, it * 2 + hf + 1)
                    nc.gpsimd.tensor_tensor(dtx_h[:, hf, :], dt_h[:, hf, :], x_h[:, hf, :], ALU.mult)\
                        .then_inc(dtx_ready, 1)
                pool.wait_ge(dtx_ready, it * 2 + 2)
                for n in range(NS):
                    pair, slot = n // 2, n // 2 % 2
                    if n % 2 == 0:
                        pool.wait_ge(bb_in[slot], it * (NS // 4 * 16) + (pair // 2 + 1) * 16)
                    for q in range(HB):
                        m = n * HB + q
                        if m >= 2:
                            pool.wait_ge(scanned, it * (NS * NB) + 2 * (m - 1))
                        nc.gpsimd.tensor_tensor(dbu[:, m % 2, :, :], dtx[:, 2 * q:2 * q + 2, :],
                                                bb[:, slot, n % 2:n % 2 + 1, :].to_broadcast([P, 2, TC]),
                                                ALU.mult).then_inc(dbu_ready, 1)
                for i in range(NB):
                    pool.wait_ge(g_free[tiles["y", i].bank], tiles["y", i].read(it))
                    nc.gpsimd.tensor_tensor(x[:, i, :], x[:, i, :], z[:, i, :], ALU.mult).then_inc(gated, 1)

        @block.scalar
        def _(act):
            act.wait_ge(alog_in, 16)
            nc.scalar.activation(aneg[:, :, :], aneg[:, :, :], ACT.Exp).then_inc(a_exp, 1)
            act.wait_ge(weights_in, 16 * N_WEIGHTS)
            act.wait_ge(consts_set, 2)
            act.wait_ge(a_set, 1)

            with act.Fori(0, CHUNKS) as it:
                act.wait_ge(hist_saved, it + 1)
                for i in range(NB):
                    t = tiles["x", i]
                    act.wait_ge(g_full, t.full(it, NG))
                    nc.scalar.activation(x[:, i, :], G[t.bank][:, :], ACT.Identity, scale=cw[:, i, KC - 1:KC],
                                         bias=cb[:, i:i + 1])
                    nc.scalar.activation(xpad[:, i, KC - 1:], G[t.bank][:, :], ACT.Copy).then_inc(g_free[t.bank], 1)
                for i in range(NB):
                    t = tiles["z", i]
                    act.wait_ge(g_full, t.full(it, NG))
                    nc.scalar.activation(z[:, i, :], G[t.bank][:, :], ACT.Silu).then_inc(g_free[t.bank], 1)
                for i in range(NB):
                    act.wait_ge(conv_step, it * (NB * (KC - 1)) + (i + 1) * (KC - 1))
                    nc.scalar.activation(x[:, i, :], x[:, i, :], ACT.Silu).then_inc(x_ready, 1)
                t = tiles["xdbl", 0]
                act.wait_ge(g_full, t.full(it, NG))
                nc.scalar.activation(xdbl[:, :], G[t.bank][0:XD, :], ACT.Copy).then_inc(g_free[t.bank], 1)
                t = tiles["ct", 0]
                act.wait_ge(g_full, t.full(it, NG))
                nc.scalar.activation(ct[:, :, :], G[t.bank][:, 0:TB * XD].rearrange("p (a e) -> p a e", e=XD),
                                     ACT.Copy).then_inc(g_free[t.bank], 1)
                for i in range(NB):
                    t = tiles["dt", i]
                    act.wait_ge(g_full, t.full(it, NG))
                    nc.scalar.activation(dtx[:, i, :], G[t.bank][:, :], ACT.Abs, bias=bdt[:, i:i + 1])
                    nc.scalar.activation(dt[:, i, :], G[t.bank][:, :], ACT.Relu, bias=bdt[:, i:i + 1])\
                        .then_inc(g_free[t.bank], 1)
                for hf in range(2):
                    t = tiles["dt", HB * hf + HB - 1]
                    act.wait_ge(g_free[t.bank], t.read(it))
                    nc.scalar.activation(t2[:, hf, :], dtx_h[:, hf, :], ACT.Exp, scale=-1.0).then_inc(e_ready, 1)
                for hf in range(2):
                    act.wait_ge(u_ready, it * 2 + hf + 1)
                    nc.scalar.activation(t3[:, hf, :], t2[:, hf, :], ACT.Ln).then_inc(l1_ready, 1)
                for hf in range(2):
                    act.wait_ge(l1_ready, it * 2 + hf + 1)
                    nc.scalar.activation(t3[:, hf, :], t3[:, hf, :], ACT.Ln)
                    nc.scalar.activation(t2[:, hf, :], t2[:, hf, :], ACT.Ln, bias=minus1[:, :]).then_inc(l23_ready, 1)
                for hf in range(2):
                    act.wait_ge(s_ready, it * 2 + hf + 1)
                    nc.scalar.activation(t3[:, hf, :], t3[:, hf, :], ACT.Exp).then_inc(log1p_ready, 1)
                for s in range(STEPS):
                    n, hf = s // 2, s % 2
                    if s < 2:
                        act.wait_ge(dt_ready, it * 2 + s + 1)
                    for j in range(HB):
                        k = s * HB + j
                        i = hf * HB + j
                        if k >= 2:
                            act.wait_ge(scanned, it * (NS * NB) + k - 1)
                        nc.scalar.activation(DA[k % 2][:, :], dt[:, i, :], ACT.Exp, scale=aneg[:, i, n:n + 1])\
                            .then_inc(decay_ready, 1)
                act.wait_ge(mv_ready, it + 1)
                nc.scalar.activation(lnv[:, :], mv[:, :, 1], ACT.Ln, bias=epsln[:, :]).then_inc(lnv_ready, 1)
                act.wait_ge(lnv_ready, it + 1)
                nc.scalar.activation(rstd[:, :], lnv[:, :], ACT.Exp, scale=-0.5).then_inc(rstd_ready, 1)

        @block.vector
        def _(dve):
            dve.wait_ge(a_exp, 1)
            nc.vector.tensor_scalar(aneg[:, :, :], aneg[:, :, :], -1.0, None, ALU.mult).then_inc(a_set, 1)
            dve.wait_ge(weights_in, 16 * N_WEIGHTS)

            def chunk(b, it):
                dve.wait_ge(hist_zero, 2 * b + 2)
                for i in range(NB):
                    t = tiles["x", i]
                    dve.wait_ge(g_free[t.bank], t.read(it))
                    for k in range(KC - 1):
                        if k:
                            dve.wait_ge(conv_step, it * (NB * (KC - 1)) + i * (KC - 1) + k)
                        nc.vector.scalar_tensor_tensor(x[:, i, :], xpad[:, i, k:k + TC], cw[:, i, k:k + 1], x[:, i, :],
                                                       ALU.mult, ALU.add).then_inc(conv_step, 1)
                dve.wait_ge(conv_step, it * (NB * (KC - 1)) + NB * (KC - 1))
                nc.vector.tensor_copy(xpad[:, :, 0:KC - 1], xpad[:, :, TC:]).then_inc(hist_saved, 1)
                for hf in range(2):
                    dve.wait_ge(e_ready, it * 2 + hf + 1)
                    nc.vector.tensor_scalar(t2[:, hf, :], t2[:, hf, :], 1.0, ONE_UP, ALU.add, ALU.max)\
                        .then_inc(u_ready, 1)
                for hf in range(2):
                    dve.wait_ge(l23_ready, it * 2 + hf + 1)
                    nc.vector.tensor_tensor(t3[:, hf, :], t3[:, hf, :], t2[:, hf, :], ALU.subtract).then_inc(s1_ready, 1)
                    dve.wait_ge(s1_ready, it * 2 + hf + 1)
                    nc.vector.tensor_tensor(t3[:, hf, :], t3[:, hf, :], dtx_h[:, hf, :], ALU.subtract)\
                        .then_inc(s_ready, 1)
                for hf in range(2):
                    dve.wait_ge(log1p_ready, it * 2 + hf + 1)
                    nc.vector.tensor_tensor(dt_h[:, hf, :], dt_h[:, hf, :], t3[:, hf, :], ALU.add).then_inc(dt_ready, 1)
                dve.wait_ge(dt_ready, it * 2 + 2)

                def add_to_y(s):
                    n, hf = s // 2, s % 2
                    for tb in range(TB):
                        q = s * TB + tb
                        dve.wait_ge(ht_full, it * (STEPS * TB) + q + 1)
                        dst = yt[:, tb, hf * 512:hf * 512 + 512]
                        c = ct[:, tb, DTR + NS + n:DTR + NS + n + 1]
                        if n == 0:
                            ins = nc.vector.tensor_scalar(dst, HT[q % 2][:, :], c, None, ALU.mult)
                        else:
                            dve.wait_ge(y_added, it * (STEPS * TB) + q - 2 * TB + 1)
                            ins = nc.vector.scalar_tensor_tensor(dst, HT[q % 2][:, :], c, dst, ALU.mult, ALU.add)
                        ins.then_inc(y_added, 1)

                for s in range(STEPS):
                    n, hf = s // 2, s % 2
                    if s >= 2:
                        dve.wait_ge(ht_full, it * (STEPS * TB) + (s - 1) * TB)
                        dve.wait_ge(carried, it * STEPS + s - 1)
                    for j in range(HB):
                        k = s * HB + j
                        i = hf * HB + j
                        dve.wait_ge(decay_ready, it * (NS * NB) + k + 1)
                        if j % 2 == 0:
                            dve.wait_ge(dbu_ready, it * (NS * HB) + k // 2 + 1)
                        nc.vector.tensor_tensor_scan(h[:, hf, j, :], DA[k % 2][:, :], dbu[:, k // 2 % 2, j % 2, :],
                                                     carry[:, n, i:i + 1], ALU.mult, ALU.add).then_inc(scanned, 1)
                    if s >= 1:
                        add_to_y(s - 1)
                    dve.wait_ge(scanned, it * (NS * NB) + (s + 1) * HB)
                    nc.vector.tensor_copy(carry[:, n, hf * HB:(hf + 1) * HB], h[:, hf, :, TC - 1]).then_inc(carried, 1)
                add_to_y(STEPS - 1)
                for i in range(NB):
                    t = tiles["y", i]
                    dve.wait_ge(g_full, t.full(it, NG))
                    nc.vector.scalar_tensor_tensor(x[:, i, :], x[:, i, :], dsk[:, i:i + 1], G[t.bank][:, :],
                                                   ALU.mult, ALU.add).then_inc(g_free[t.bank], 1)
                dve.wait_ge(x_in, it * 16 + 16)
                for tb in range(TB):
                    t = tiles["o", tb]
                    dve.wait_ge(g_full, t.full(it, NG))
                    nc.vector.tensor_tensor(xres[:, tb, :], G[t.bank][:, :], xres[:, tb, :], ALU.add)\
                        .then_inc(g_free[t.bank], 1)
                for tb in range(TB):
                    t = tiles["o", tb]
                    dve.wait_ge(g_free[t.bank], t.read(it))
                    nc.vector.bn_stats(stats[:, tb, :], xres[:, tb, :]).then_inc(stats_ready, 1)
                dve.wait_ge(stats_ready, it * TB + TB)
                dve.sem_inc(stats_seen, 1)
                for tb in range(TB):
                    ins = nc.vector.bn_aggr(mv[:, tb, :], stats[:, tb, :])
                ins.then_inc(mv_ready, 1)
                dve.wait_ge(rstd_ready, it + 1)
                for tb in range(TB):
                    ins = nc.vector.tensor_scalar(xres[:, tb, :], xres[:, tb, :], mv[:, tb, 0:1], rstd[:, tb:tb + 1],
                                                  ALU.subtract, ALU.mult)
                ins.then_inc(x1_ready, 1)

            with dve.Fori(0, BATCH) as b:
                dve.wait_ge(hist_saved, b * CPB + 1)
                nc.vector.memset(xpad[:, :, 0:KC - 1], 0.0).then_inc(hist_zero, 1)
                nc.vector.memset(carry[:, :, :], 0.0).then_inc(hist_zero, 1)
                with dve.Fori(0, CPB) as c:
                    chunk(b, b * CPB + c)

        @block.tensor
        def _(pe):
            pe.wait_ge(weights_in, 16 * N_WEIGHTS)
            pe.wait_ge(ident_set, 1)

            with pe.Fori(0, CHUNKS) as it:
                def room(t):
                    pe.wait_ge(g_free[t.bank], t.empty(it))
                    return G[t.bank]

                pe.wait_ge(xt_in, it * 16 + 16)
                for part, first in (("x", 0), ("z", DI)):
                    for i in range(NB):
                        bank = room(tiles[part, i])
                        for k in range(KM):
                            ins = nc.tensor.matmul(bank[:, :], win[:, k, first + i * P:first + (i + 1) * P],
                                                   xt[:, k, :], start=(k == 0), stop=(k == KM - 1))
                        ins.then_inc(g_full, 1)
                bank = room(tiles["xdbl", 0])
                for i in range(NB):
                    pe.wait_ge(x_ready, it * NB + i + 1)
                    ins = nc.tensor.matmul(bank[0:XD, :], wxp[:, i, :], x[:, i, :], start=(i == 0), stop=(i == NB - 1))
                ins.then_inc(g_full, 1)
                t = tiles["xdbl", 0]
                pe.wait_ge(g_free[t.bank], t.read(it))
                bank = room(tiles["ct", 0])
                for tb in range(TB):
                    ins = nc.tensor.transpose(bank[:, tb * XD:(tb + 1) * XD], xdbl[:, tb * P:(tb + 1) * P],
                                              ident[0:XD, 0:XD])
                ins.then_inc(g_full, 1)
                for i in range(NB):
                    bank = room(tiles["dt", i])
                    nc.tensor.matmul(bank[:, :], wdt[:, i * P:(i + 1) * P], xdbl[0:DTR, :], start=True, stop=True)\
                        .then_inc(g_full, 1)
                for s in range(STEPS):
                    hf = s % 2
                    pe.wait_ge(scanned, it * (NS * NB) + (s + 1) * HB)
                    for tb in range(TB):
                        q = s * TB + tb
                        if q >= 2:
                            pe.wait_ge(y_added, it * (STEPS * TB) + q - 1)
                        for j in range(HB):
                            ins = nc.tensor.transpose(HT[q % 2][:, j * P:(j + 1) * P],
                                                      h[:, hf, j, tb * P:(tb + 1) * P], ident[:, :])
                        ins.then_inc(ht_full, 1)
                pe.wait_ge(y_added, it * (STEPS * TB) + STEPS * TB)
                for i in range(NB):
                    bank = room(tiles["y", i])
                    for tb in range(TB):
                        ins = nc.tensor.transpose(bank[:, tb * P:(tb + 1) * P], yt[:, tb, i * P:(i + 1) * P],
                                                  ident[:, :])
                    ins.then_inc(g_full, 1)
                pe.wait_ge(gated, it * NB + NB)
                for tb in range(TB):
                    bank = room(tiles["o", tb])
                    for i in range(NB):
                        ins = nc.tensor.matmul(bank[:, :], x[:, i, tb * P:(tb + 1) * P], wout[:, i, :],
                                               start=(i == 0), stop=(i == NB - 1))
                    ins.then_inc(g_full, 1)


def ffn_phase(nc, x1, w1, b1, w2, b2, out):
    ctx = ExitStack()
    with ctx:
        def sb(name, shape, dt=F32):
            return ctx.enter_context(nc.sbuf_tensor(name, shape, dt))

        def sem(name):
            return ctx.enter_context(nc.semaphore(name))

        w1q = sb("w1q", [P, KM, DFF], F32R)
        w2q = sb("w2q", [P, NJ, DM], F32R)
        raw = sb("raw", [P, 2, KM * DFF])
        below = sb("below", [P, DFF])
        ident = sb("ident2", [P, P])
        ones = sb("ones", [P, P])
        sums = sb("sums", [P, 2])
        thr = sb("thr", [P, 2, 2])
        b1c = sb("b1c", [P, NJ])
        b2r = sb("b2r", [P, DM])
        epsln = sb("epsln2", [P, 1])
        xr = sb("xr", [P, 2, TB, DM])
        xhi = sb("xhi", [P, KM, TC], F32R)
        xlo = sb("xlo", [P, KM, TC], F32R)
        hr = sb("hr", [P, 2, TC])
        hhi = sb("hhi", [P, 2, TC], F32R)
        hlo = sb("hlo", [P, 2, TC], F32R)
        stats = sb("stats2", [P, TB, 6])
        mv = sb("mv2", [P, TB, 2])
        lnv = sb("lnv2", [P, TB])
        rstd = sb("rstd2", [P, TB])

        XT = [ctx.enter_context(nc.psum_tensor(f"xt_ps{i}", [P, TC], F32)) for i in range(2)]
        HP = [ctx.enter_context(nc.psum_tensor(f"hidden_ps{i}", [P, TC], F32)) for i in range(2)]
        OP = [ctx.enter_context(nc.psum_tensor(f"out_ps{i}", [P, DM], F32)) for i in range(TB)]

        raw_in = sem("raw_in")
        raw2_in = sem("raw2_in")
        bias_in = sem("bias_in")
        consts_set = sem("consts_set2")
        ident_zero = sem("ident_zero2")
        ident_set = sem("ident_set2")
        sums_ready = sem("sums_ready")
        total_ready = sem("total_ready")
        thr_step = sem("thr_step")
        below_ready = sem("below_ready")
        quantised = sem("quantised")
        x_in = [sem("xr_in0"), sem("xr_in1")]
        xt_full = sem("xt_full")
        hi_ready = sem("hi_ready")
        lo_ready = sem("lo_ready")
        hp_full = sem("hp_full")
        relu_done = sem("relu_done")
        hhi_ready = sem("hhi_ready")
        hlo_ready = sem("hlo_ready")
        h_used = sem("h_used")
        res_ready = sem("res_ready")
        added = sem("added")
        stats_ready = sem("stats_ready2")
        stats_seen = sem("stats_seen2")
        mv_ready = sem("mv_ready2")
        lnv_ready = sem("lnv_ready2")
        rstd_ready = sem("rstd_ready2")
        y_ready = sem("y_ready")
        stored = [sem("stored0"), sem("stored1")]

        block = ctx.enter_context(nc.Block())
        PAIRS = CHUNKS // 2

        @block.sync
        def _(sp):
            sp.dma_start(raw[:, 0, :].rearrange("p (k f) -> p k f", k=KM), w1.rearrange("(k p) f -> p k f", p=P))\
                .then_inc(raw_in, 16)
            sp.dma_start(raw[:, 1, :].rearrange("p (j e) -> p j e", j=NJ), w2.rearrange("(j p) e -> p j e", p=P))\
                .then_inc(raw2_in, 16)
            sp.dma_start(b1c[:, :], b1).then_inc(bias_in, 16)
            sp.dma_start(b2r[:, :], b2.rearrange("(o e) -> o e", o=1).to_broadcast([P, DM])).then_inc(bias_in, 16)

            def load(first, par):
                sp.dma_start(xr[:, par, :, :], x1[bass.ds(first, TC), :].rearrange("(a p) e -> p a e", p=P))\
                    .then_inc(x_in[par], 16)

            def store(it, first, par):
                sp.wait_ge(y_ready, it + 1)
                sp.dma_start(out[bass.ds(first, TC), :].rearrange("(a p) e -> p a e", p=P), xr[:, par, :, :])\
                    .then_inc(stored[par], 16)

            load(0, 0)
            load(TC, 1)
            with sp.Fori(0, PAIRS - 1) as i:
                firsts = [sp.snap(i * (2 * TC) + par * TC) for par in range(4)]
                for par in range(2):
                    store(2 * i + par, firsts[par], par)
                    sp.wait_ge(stored[par], i * 16 + 16)
                    load(firsts[par + 2], par)
            for par in range(2):
                store(CHUNKS - 2 + par, (CHUNKS - 2 + par) * TC, par)
            for par in range(2):
                sp.wait_ge(stored[par], PAIRS * 16)

        @block.gpsimd
        def _(pool):
            nc.gpsimd.memset(epsln[:, :], EPS_LN).then_inc(consts_set, 1)
            nc.gpsimd.memset(ones[:, :], 1.0).then_inc(consts_set, 1)
            nc.gpsimd.memset(ident[:, :], 0.0).then_inc(ident_zero, 1)
            pool.wait_ge(ident_zero, 1)
            nc.gpsimd.affine_select(out=ident[:, :], in_=ident[:, :], compare_op=ALU.not_equal, fill=1.0,
                                    base=0, pattern=[[-1, P]], channel_multiplier=1).then_inc(ident_set, 1)
            pool.sem_inc(added, TB)

        def chunk_order(eng, body):
            with eng.Fori(0, PAIRS - 1) as i:
                for par in range(2):
                    body(i, 2 * i + par, par, False)
            body(PAIRS - 1, CHUNKS - 2, 0, False)
            body(PAIRS - 1, CHUNKS - 1, 1, True)

        @block.scalar
        def _(act):
            act.wait_ge(bias_in, 32)
            act.wait_ge(consts_set, 2)

            def split_hi(it):
                for k in range(KM):
                    act.wait_ge(xt_full, it * KM + k + 1)
                    nc.scalar.activation(xhi[:, k, :], XT[k % 2][:, :], ACT.Copy).then_inc(hi_ready, 1)

            split_hi(0)

            def chunk(i, it, par, last):
                for j in range(NJ):
                    act.wait_ge(hp_full, it * NJ + j + 1)
                    if j >= 2:
                        act.wait_ge(hlo_ready, it * NJ + j - 1)
                    nc.scalar.activation(hr[:, j % 2, :], HP[j % 2][:, :], ACT.Relu, bias=b1c[:, j:j + 1])\
                        .then_inc(relu_done, 1)
                if not last:
                    split_hi(it + 1)
                act.wait_ge(mv_ready, it + 1)
                nc.scalar.activation(lnv[:, :], mv[:, :, 1], ACT.Ln, bias=epsln[:, :]).then_inc(lnv_ready, 1)
                act.wait_ge(lnv_ready, it + 1)
                nc.scalar.activation(rstd[:, :], lnv[:, :], ACT.Exp, scale=-0.5).then_inc(rstd_ready, 1)

            chunk_order(act, chunk)

        @block.vector
        def _(dve):
            dve.wait_ge(raw_in, 16)
            nc.vector.tensor_reduce(sums[:, 0:1], raw[:, 0, :], AX.X, ALU.add, apply_absolute_value=True)\
                .then_inc(sums_ready, 1)
            dve.wait_ge(raw2_in, 16)
            nc.vector.tensor_reduce(sums[:, 1:2], raw[:, 1, :], AX.X, ALU.add, apply_absolute_value=True)\
                .then_inc(sums_ready, 1)
            dve.wait_ge(total_ready, 1)
            nc.vector.tensor_scalar(thr[:, :, 0], XT[0][:, 0:2], 0.5 / (DFF * DM), 0.5 * EPS_Q, ALU.mult, ALU.add)\
                .then_inc(thr_step, 1)
            dve.wait_ge(thr_step, 1)
            nc.vector.tensor_scalar(thr[:, :, 1], thr[:, :, 0], -1.0, None, ALU.mult).then_inc(thr_step, 1)
            dve.wait_ge(thr_step, 2)
            for w in range(2):
                wq = (w1q if w == 0 else w2q)[:, :, :].rearrange("p a b -> p (a b)")
                for c in range(KM):
                    part = slice(c * DFF, (c + 1) * DFF)
                    n = w * KM + c
                    if n:
                        dve.wait_ge(quantised, n)
                    nc.vector.tensor_scalar(below[:, :], raw[:, w, part], thr[:, w, 1:2], None, ALU.is_lt)\
                        .then_inc(below_ready, 1)
                    dve.wait_ge(below_ready, n + 1)
                    nc.vector.scalar_tensor_tensor(wq[:, part], raw[:, w, part], thr[:, w, 0:1], below[:, :],
                                                   ALU.is_gt, ALU.subtract).then_inc(quantised, 1)

            def split_lo(it):
                for k in range(KM):
                    dve.wait_ge(hi_ready, it * KM + k + 1)
                    nc.vector.tensor_tensor(xlo[:, k, :], XT[k % 2][:, :], xhi[:, k, :].bitcast(F32), ALU.subtract)\
                        .then_inc(lo_ready, 1)

            split_lo(0)

            def chunk(i, it, par, last):
                for j in range(NJ):
                    dve.wait_ge(relu_done, it * NJ + j + 1)
                    if j >= 2:
                        dve.wait_ge(h_used, it * NJ + j - 1)
                    nc.vector.tensor_copy(hhi[:, j % 2, :], hr[:, j % 2, :]).then_inc(hhi_ready, 1)
                    dve.wait_ge(hhi_ready, it * NJ + j + 1)
                    nc.vector.tensor_tensor(hlo[:, j % 2, :], hr[:, j % 2, :], hhi[:, j % 2, :].bitcast(F32),
                                            ALU.subtract).then_inc(hlo_ready, 1)
                    if j >= 8 and j < 8 + TB:
                        tb = j - 8
                        nc.vector.tensor_tensor(xr[:, par, tb, :], xr[:, par, tb, :], b2r[:, :], ALU.add)\
                            .then_inc(res_ready, 1)
                if not last:
                    split_lo(it + 1)
                dve.wait_ge(h_used, it * NJ + NJ)
                dve.wait_ge(res_ready, it * TB + TB)
                for tb in range(TB):
                    nc.vector.tensor_tensor(xr[:, par, tb, :], OP[tb][:, :], xr[:, par, tb, :], ALU.add).then_inc(added, 1)
                for tb in range(TB):
                    dve.wait_ge(added, it * TB + TB + tb + 1)
                    nc.vector.bn_stats(stats[:, tb, :], xr[:, par, tb, :]).then_inc(stats_ready, 1)
                dve.wait_ge(stats_ready, it * TB + TB)
                dve.sem_inc(stats_seen, 1)
                for tb in range(TB):
                    ins = nc.vector.bn_aggr(mv[:, tb, :], stats[:, tb, :])
                ins.then_inc(mv_ready, 1)
                dve.wait_ge(rstd_ready, it + 1)
                for tb in range(TB):
                    ins = nc.vector.tensor_scalar(xr[:, par, tb, :], xr[:, par, tb, :], mv[:, tb, 0:1],
                                                  rstd[:, tb:tb + 1], ALU.subtract, ALU.mult)
                ins.then_inc(y_ready, 1)

            chunk_order(dve, chunk)

        @block.tensor
        def _(pe):
            pe.wait_ge(consts_set, 2)
            pe.wait_ge(sums_ready, 2)
            nc.tensor.matmul(XT[0][:, 0:2], ones[:, :], sums[:, :], start=True, stop=True).then_inc(total_ready, 1)
            pe.wait_ge(ident_set, 1)
            pe.wait_ge(quantised, 2 * KM)

            def transposes(it, par, i, blocks):
                pe.wait_ge(x_in[par], i * 16 + 16)
                for k in blocks:
                    if k >= 2:
                        pe.wait_ge(lo_ready, it * KM + k - 1)
                    for tb in range(TB):
                        ins = nc.tensor.transpose(XT[k % 2][:, tb * P:(tb + 1) * P],
                                                  xr[:, par, tb, k * P:(k + 1) * P], ident[:, :])
                    ins.then_inc(xt_full, 1)

            transposes(0, 0, 0, range(KM))

            def chunk(i, it, par, last):
                def up(j):
                    if j >= 2:
                        pe.wait_ge(relu_done, it * NJ + j - 1)
                    for k in range(KM):
                        for part in (xhi, xlo):
                            ins = nc.tensor.matmul(HP[j % 2][:, :], w1q[:, k, j * P:(j + 1) * P], part[:, k, :],
                                                   start=(k == 0 and part is xhi), stop=(k == KM - 1 and part is xlo))
                    ins.then_inc(hp_full, 1)

                def down(j):
                    pe.wait_ge(hlo_ready, it * NJ + j + 1)
                    for tb in range(TB):
                        if j == 0:
                            pe.wait_ge(added, it * TB + tb + 1)
                        for part in (hhi, hlo):
                            ins = nc.tensor.matmul(OP[tb][:, :], part[:, j % 2, tb * P:(tb + 1) * P], w2q[:, j, :],
                                                   start=(j == 0 and part is hhi), stop=(j == NJ - 1 and part is hlo))
                    ins.then_inc(h_used, 1)

                pe.wait_ge(lo_ready, it * KM + KM)
                up(0)
                for j in range(NJ):
                    if j + 1 < NJ:
                        up(j + 1)
                    if j == NJ - 2 and not last:
                        transposes(it + 1, 1 - par, i + par, range(2))
                    down(j)
                    if j == NJ - 2 and not last:
                        transposes(it + 1, 1 - par, i + par, range(2, KM))

            chunk_order(pe, chunk)


def build(nc, x_tm, x_cm, w_in, conv_w, conv_b, w_xp, w_dt, b_dt, a_log, d_skip, w_out, w1, b1, w2, b2, out):
    b_rows = nc.dram_tensor("b_rows", [NS, TC], F32, kind="Internal").ap()
    x1 = nc.dram_tensor("x1", [BATCH * SEQ, DM], F32, kind="Internal").ap()
    mixer_phase(nc, x_tm, x_cm, w_in, conv_w, conv_b, w_xp, w_dt, b_dt, a_log, d_skip, w_out, b_rows, x1)
    ffn_phase(nc, x1, w1, b1, w2, b2, out)


def kernel(L0_attn_hidden_states, L0_attn_in_proj_w, L0_attn_conv_w, L0_attn_conv_b, L0_attn_x_proj_w,
           L0_attn_dt_proj_w, L0_attn_dt_proj_b, L0_attn_A_log, L0_attn_D, L0_attn_out_proj_w,
           L0_ffn_W1, L0_ffn_b1, L0_ffn_W2, L0_ffn_b2):
    import numpy as np
    import concourse.bacc as bacc
    from concourse.bass_utils import run_bass_kernel_spmd

    tokens = np.asarray(L0_attn_hidden_states).reshape(BATCH * SEQ, DM)
    arrays = {
        "x_tm": tokens,
        "x_cm": tokens.T,
        "w_in": np.asarray(L0_attn_in_proj_w).T,
        "conv_w": np.asarray(L0_attn_conv_w).reshape(NB, P, KC).transpose(1, 0, 2),
        "conv_b": np.asarray(L0_attn_conv_b).reshape(NB, P).T,
        "w_xp": np.asarray(L0_attn_x_proj_w).T,
        "w_dt": np.asarray(L0_attn_dt_proj_w).T,
        "b_dt": np.asarray(L0_attn_dt_proj_b).reshape(NB, P).T,
        "a_log": np.asarray(L0_attn_A_log).reshape(NB, P, NS).transpose(1, 0, 2),
        "d_skip": np.asarray(L0_attn_D).reshape(NB, P).T,
        "w_out": np.asarray(L0_attn_out_proj_w).T,
        "w1": np.asarray(L0_ffn_W1).T,
        "b1": np.asarray(L0_ffn_b1).reshape(NJ, P).T,
        "w2": np.asarray(L0_ffn_W2).T,
        "b2": L0_ffn_b2,
    }
    arrays = {name: np.ascontiguousarray(a) for name, a in arrays.items()}
    nc = bacc.Bacc("TRN2", target_bir_lowering=False, num_devices=1)
    args = [nc.dram_tensor(name, a.shape, F32, kind="ExternalInput").ap() for name, a in arrays.items()]
    out = nc.dram_tensor("out", [BATCH * SEQ, DM], F32, kind="ExternalOutput").ap()
    build(nc, *args, out)
    r = run_bass_kernel_spmd(nc, [arrays], core_ids=[0])
    return np.asarray(r.results[0]["out"]).reshape(BATCH, SEQ, DM)
```

```python
from contextlib import ExitStack

import concourse.bass as bass
from concourse import mybir

F32 = mybir.dt.float32
F32R = mybir.dt.float32r
ALU = mybir.AluOpType
ACT = mybir.ActivationFunctionType
AX = mybir.AxisListType

P = 128
BATCH, SEQ, DM = 2, 4096, 512
DI, NS, KC, DTR = 1024, 16, 4, 64
DFF = 2048
TC = 512
CHUNKS = BATCH * SEQ // TC
CPB = SEQ // TC
NB = DI // P
KM = DM // P
TB = TC // P
HB = NB // 2
XD = DTR + 2 * NS
NJ = DFF // P
EPS_LN = 1e-5
EPS_Q = 1e-5
ONE_UP = 1.0 + 2.0 ** -23

STEPS = 2 * NS


class Chunk:

    def __init__(self, i, j, bases=None):
        self.i, self.j, self.par, self.bases = i, j, j % 2, bases

    def count(self, per_chunk, count):
        base = self.bases[per_chunk] if self.bases else self.i * (2 * per_chunk)
        return base + (self.j * per_chunk + count)

    def token(self):
        return self.i * TC + (self.par * SEQ + self.j // 2 * TC)

    def near(self, d):
        return Chunk(self.i, self.j + d, self.bases)


def wait(eng, sem, chunk, per_chunk, count):
    value = chunk.count(per_chunk, count)
    if not isinstance(value, int) or value > 0:
        eng.wait_ge(sem, value)


def walk(eng, body):
    body(Chunk(0, 0), True, False)
    with eng.Fori(0, CHUNKS // 2 - 1) as i:
        bases = {n: eng.snap(i * (2 * n)) for n in (1, 4, 8, 16, 32, 64, 128)}
        for j in (1, 2):
            body(Chunk(i, j, bases), False, False)
    body(Chunk(CHUNKS // 2 - 1, 1), False, True)


KINDS = {"x": NB, "z": NB, "xd": 1, "ct": 1, "dt": NB, "y": NB, "o": TB}

CONV_STEP = 16
SLOTS = {}
for _tb in range(TB):
    for _s in range(8):
        SLOTS[_s, _tb] = [("x", _s, (_tb,))]
    for _s in range(8, 16):
        SLOTS[_s, _tb] = [("o", (_s - 8) // 2, (_s % 2 * TB + _tb,))]
SLOTS[CONV_STEP, 1] = [("z", 0, tuple(range(KM))), ("z", 1, tuple(range(KM))), ("xd", 0, tuple(range(NB)))]
SLOTS[17, 0] = [("ct", 0, ())]
DT_AT = {17: (0,), 18: (1, 2), 19: (3, 4), 20: (5, 6), 21: (7,)}
for _s, _tiles in DT_AT.items():
    for _n, _i in enumerate(_tiles):
        SLOTS.setdefault((_s, _n), []).append(("dt", _i, ()))
Z_AT = {22: 2, 23: 3, 24: 4, 25: 5, 26: 6, 28: 7}
for _s, _i in Z_AT.items():
    for _tb in range(TB):
        SLOTS[_s, _tb] = [("z", _i, (_tb,))]
LN_STEP = 23
Z_SILU_STEP = STEPS - 1
SP_STEP = {19 + 2 * q: q for q in range(4)}
CONV_DONE = [(i // 2) * 2 * KC + 2 * (KC - 1) + i % 2 + 1 for i in range(NB)]
RESIDUAL_STEP = {10 + 2 * tb: tb for tb in range(TB)}


def banks():
    order = [("y", i) for i in range(NB)]
    for s in range(STEPS):
        for tb in range(TB):
            for kind, i, _ in SLOTS.get((s, tb), []):
                if (kind, i) not in order:
                    order.append((kind, i))
    return {name: n % 2 for n, name in enumerate(order)}


BANK = banks()


def mixer_phase(nc, x_tm, x_cm, w_in, conv_w, conv_b, w_xp, w_dt, b_dt, a_log, d_skip, w_out, b_rows, x1):
    ctx = ExitStack()
    with ctx:
        def sb(name, shape, dt=F32):
            return ctx.enter_context(nc.sbuf_tensor(name, shape, dt))

        def sem(name):
            return ctx.enter_context(nc.semaphore(name))

        win = sb("win", [P, 2, KM, P])
        wout = sb("wout", [P, NB, DM])
        wxp = sb("wxp", [P, NB, XD])
        wdt = sb("wdt", [DTR, DI])
        ident = sb("ident", [P, P])
        cw = sb("cw", [P, NB, KC])
        cb = sb("cb", [P, NB])
        bdt = sb("bdt", [P, NB])
        dsk = sb("dsk", [P, NB])
        aneg = sb("aneg", [P, NB, NS])
        minus1 = sb("minus1", [P, 1])
        ones = sb("ones_hb", [P, HB])
        epsln = sb("epsln", [P, 1])
        xt = sb("xt", [P, KM, TC])
        xres = sb("xres", [P, TB, DM])
        xpad = sb("xpad", [P, NB, KC - 1 + TC])
        hist = sb("hist", [P, 2, NB, KC - 1])
        x = sb("x", [P, 2, NB, TC])
        z = sb("z", [P, NB, TC])
        dt = sb("dt", [P, 2, NB, TC])
        dtx = sb("dtx", [P, NB, TC])
        yt = sb("yt", [P, TB, DI])
        bb = sb("bb", [P, 2, TC])
        dbu = sb("dbu", [P, 2, 2, TC])
        h = sb("h", [P, 2, HB, TC])
        carry = sb("carry", [P, 2, NS, NB])
        xdbl = sb("xdbl", [XD, TC])
        ct = sb("ct", [P, 2, TB, XD])
        stats = sb("stats", [P, TB, 6])
        mv = sb("mv", [P, TB, 2])
        lnv = sb("lnv", [P, TB])
        rstd = sb("rstd", [P, TB])

        def quarter(q):
            return slice(2 * q, 2 * q + 2)

        def t2(q):
            return xpad[:, 2 * (q % 2):2 * (q % 2) + 2, KC - 1:]

        def t3(q):
            return xpad[:, HB + 2 * (q % 2):HB + 2 * (q % 2) + 2, KC - 1:]

        G = [ctx.enter_context(nc.psum_tensor(f"gemm{i}", [P, 512], F32)) for i in range(2)]
        DA = [ctx.enter_context(nc.psum_tensor(f"decay{i}", [P, TC], F32)) for i in range(4)]
        HT = [ctx.enter_context(nc.psum_tensor(f"ht{i}", [P, 512], F32)) for i in range(2)]

        weights_in = sem("weights_in")
        alog_in = sem("alog_in")
        win_in = {kind: [sem(f"win_{kind}{i}") for i in range(2)] for kind in "xz"}
        xt_in = {kind: sem(f"xt_{kind}_in") for kind in "xz"}
        x_in = sem("x_in")
        b_out = sem("b_out")
        bb_in = [sem("bb_in0"), sem("bb_in1")]
        x1_out = sem("x1_out")
        consts_set = sem("consts_set")
        ident_zero = sem("ident_zero")
        ident_set = sem("ident_set")
        a_exp = sem("a_exp")
        a_set = sem("a_set")
        full = {kind: sem(f"{kind}_full") for kind in KINDS}
        read = {kind: sem(f"{kind}_read") for kind in KINDS}
        state_zero = sem("state_zero")
        hist_put = sem("hist_put")
        hist_saved = sem("hist_saved")
        conv_step = sem("conv_step")
        x_ready = sem("x_ready")
        z_ready = sem("z_ready")
        abs_ready = sem("abs_ready")
        e_ready = sem("e_ready")
        u_ready = sem("u_ready")
        l1_ready = sem("l1_ready")
        l23_ready = sem("l23_ready")
        s1_ready = sem("s1_ready")
        abs2_ready = sem("abs2_ready")
        s_ready = sem("s_ready")
        log1p_ready = sem("log1p_ready")
        dt_ready = sem("dt_ready")
        dtx_ready = sem("dtx_ready")
        decay_ready = sem("decay_ready")
        dbu_ready = sem("dbu_ready")
        scanned = sem("scanned")
        carried = sem("carried")
        ht_full = sem("ht_full")
        y_added = sem("y_added")
        gated = sem("gated")
        stats_ready = sem("stats_ready")
        stats_seen = sem("stats_seen")
        mv_ready = sem("mv_ready")
        lnv_ready = sem("lnv_ready")
        rstd_ready = sem("rstd_ready")
        x1_ready = sem("x1_ready")

        N_WEIGHTS = 7
        SCANS = NS * NB
        DBUS = NS * HB
        ADDS = STEPS * TB

        def wait_full(eng, kind, chunk, i):
            wait(eng, full[kind], chunk, KINDS[kind], i + 1)

        def wait_read(eng, kind, chunk, i):
            wait(eng, read[kind], chunk, KINDS[kind], i + 1)

        block = ctx.enter_context(nc.Block())

        @block.sync
        def _(sp):
            def load_xt(token, kind):
                sp.dma_start(xt[:, :, :], x_cm.rearrange("(k p) t -> p k t", p=P)[:, :, bass.ds(token, TC)])\
                    .then_inc(xt_in[kind], 16)

            def load_win(kind, i):
                block_of = i + (NB if kind == "z" else 0)
                sp.dma_start(win[:, i % 2, :, :], w_in[block_of]).then_inc(win_in[kind][i % 2], 16)

            def load_bb(c, n):
                wait(sp, dbu_ready, c, DBUS, (n - 1) * HB)
                sp.dma_start(bb[:, n % 2, :], b_rows[c.par, n:n + 1, :].to_broadcast([P, TC])).then_inc(bb_in[n % 2], 16)

            def store_b(f):
                wait_read(sp, "xd", f, 0)
                sp.dma_start(b_rows[f.par, :, :], xdbl[DTR:DTR + NS, :]).then_inc(b_out, 16)

            def store_x1(p, token):
                wait(sp, x1_ready, p, 1, 1)
                sp.dma_start(x1[bass.ds(token, TC), :].rearrange("(a p) e -> p a e", p=P), xres[:, :, :])\
                    .then_inc(x1_out, 16)

            def load_x(p, token):
                wait(sp, x1_out, p, 16, 0)
                sp.dma_start(xres[:, :, :], x_tm[bass.ds(token, TC), :].rearrange("(a p) e -> p a e", p=P))\
                    .then_inc(x_in, 16)

            first = Chunk(0, 0)
            load_xt(0, "x")
            load_win("x", 0)
            load_win("x", 1)
            sp.dma_start(cw[:, :, :], conv_w).then_inc(weights_in, 16)
            for dst, src in ((cb, conv_b), (bdt, b_dt), (dsk, d_skip)):
                sp.dma_start(dst[:, :], src).then_inc(weights_in, 16)
            sp.dma_start(aneg[:, :, :], a_log).then_inc(alog_in, 16)
            sp.dma_start(wxp[:, :, :], w_xp.rearrange("(i p) e -> p i e", p=P)).then_inc(weights_in, 16)
            sp.dma_start(wdt[:, :], w_dt).then_inc(weights_in, 16)
            sp.dma_start(wout[:, :, :], w_out.rearrange("(i p) e -> p i e", p=P)).then_inc(weights_in, 16)
            for i in range(2, NB):
                wait_full(sp, "x", first, i - 2)
                load_win("x", i)
            store_b(first)

            def chunk(c, is_first, is_last):
                p, f = c.near(-1), c.near(1)
                fixed = isinstance(c.i, int)
                tok_c, tok_f, tok_p = (t if fixed else sp.snap(t) for t in (c.token(), f.token(), p.token()))
                if not is_last:
                    if is_first:
                        wait_full(sp, "x", c, NB - 1)
                    else:
                        wait_full(sp, "z", p, NB - 1)
                    load_xt(tok_f, "x")
                    load_win("x", 0)
                    load_win("x", 1)
                wait(sp, b_out, c, 16, 16)
                load_bb(c, 0)
                load_bb(c, 1)
                if not is_first:
                    load_x(p, tok_p)
                if not is_last:
                    for i in range(2, NB):
                        wait_full(sp, "x", f, i - 2)
                        load_win("x", i)
                        if i % 2 == 0:
                            load_bb(c, i // 2 + 1)
                    wait_full(sp, "x", f, NB - 1)
                else:
                    for n in range(2, 5):
                        load_bb(c, n)
                    wait_full(sp, "z", p, NB - 1)
                load_xt(tok_c, "z")
                load_win("z", 0)
                load_win("z", 1)
                for n in range(5, 10):
                    load_bb(c, n)
                for i in (2, 3):
                    wait_full(sp, "z", c, i - 2)
                    load_win("z", i)
                if not is_last:
                    store_b(f)
                load_bb(c, 10)
                for i, n in ((4, 11), (5, 12), (6, 13), (7, 14)):
                    load_bb(c, n)
                    wait_full(sp, "z", c, i - 2)
                    load_win("z", i)
                load_bb(c, 15)
                if not is_first:
                    store_x1(p, tok_p)

            walk(sp, chunk)
            last = Chunk(CHUNKS // 2 - 1, 1)
            load_x(last, last.token())
            store_x1(last, last.token())
            wait(sp, x1_out, last, 16, 16)

        @block.gpsimd
        def _(pool):
            nc.gpsimd.memset(ones[:, :], 1.0).then_inc(consts_set, 1)
            nc.gpsimd.memset(minus1[:, :], -1.0).then_inc(consts_set, 1)
            nc.gpsimd.memset(epsln[:, :], EPS_LN).then_inc(consts_set, 1)
            nc.gpsimd.memset(ident[:, :], 0.0).then_inc(ident_zero, 1)
            pool.wait_ge(consts_set, 3)
            pool.wait_ge(ident_zero, 1)
            nc.gpsimd.affine_select(out=ident[:, :], in_=ident[:, :], compare_op=ALU.not_equal, fill=1.0,
                                    base=0, pattern=[[-1, P]], channel_multiplier=1).then_inc(ident_set, 1)

            def gate(p, i):
                if i == 0:
                    wait(pool, z_ready, p, NB, NB)
                wait_read(pool, "y", p, i)
                nc.gpsimd.tensor_tensor(x[:, p.par, i, :], x[:, p.par, i, :], z[:, i, :], ALU.mult).then_inc(gated, 1)

            def save_state(c, s):
                n, hf = s // 2, s % 2
                wait(pool, scanned, c, SCANS, (s + 1) * HB)
                last = h[:, hf, :, TC - 1]
                nc.gpsimd.tensor_tensor(carry[:, c.par, n, hf * HB:(hf + 1) * HB], last, ones[:, :], ALU.mult)\
                    .then_inc(carried, 1)

            def chunk(c, is_first, is_last):
                for s in range(STEPS):
                    n, hf = s // 2, s % 2
                    if s >= 2:
                        save_state(c, s - 2)
                    elif not is_first:
                        save_state(c.near(-1), STEPS - 2 + s)
                    if hf == 0:
                        wait(pool, bb_in[n % 2], c, NS // 2 * 16, (n // 2 + 1) * 16)
                    for q in (2 * hf, 2 * hf + 1):
                        m = n * HB + q
                        if n == 0:
                            wait(pool, dtx_ready, c, 4, q + 1)
                        wait(pool, scanned, c, SCANS, 2 * (m - 1))
                        nc.gpsimd.tensor_tensor(dbu[:, m % 2, :, :], dtx[:, quarter(q), :],
                                                bb[:, n % 2:n % 2 + 1, :].to_broadcast([P, 2, TC]),
                                                ALU.mult).then_inc(dbu_ready, 1)
                    if 1 <= s <= NB and not is_first:
                        gate(c.near(-1), s - 1)

            walk(pool, chunk)
            for i in range(NB):
                gate(Chunk(CHUNKS // 2 - 1, 1), i)

        @block.scalar
        def _(act):
            act.wait_ge(alog_in, 16)
            nc.scalar.activation(aneg[:, :, :], aneg[:, :, :], ACT.Exp).then_inc(a_exp, 1)
            act.wait_ge(weights_in, 16 * N_WEIGHTS)
            act.wait_ge(consts_set, 3)
            act.wait_ge(a_set, 1)


            def decay(c, s, j):
                n, hf = s // 2, s % 2
                k = s * HB + j
                i = hf * HB + j
                if n == 0 and j % 2 == 0:
                    wait(act, dt_ready, c, 4, i // 2 + 1)
                wait(act, scanned, c, SCANS, k - 3)
                nc.scalar.activation(DA[k % 4][:, :], dt[:, c.par, i, :], ACT.Exp, scale=aneg[:, i, n:n + 1])\
                    .then_inc(decay_ready, 1)

            def take_x(f, i):
                wait_full(act, "x", f, i)
                nc.scalar.activation(xpad[:, i, KC - 1:], G[BANK["x", i]][:, :], ACT.Copy).then_inc(read["x"], 1)

            def silu_x(f, blocks):
                for i in blocks:
                    wait(act, conv_step, f, NB * KC, CONV_DONE[i])
                    nc.scalar.activation(x[:, f.par, i, :], x[:, f.par, i, :], ACT.Silu).then_inc(x_ready, 1)

            def take_xd(f):
                wait_full(act, "xd", f, 0)
                nc.scalar.activation(xdbl[:, :], G[BANK["xd", 0]][0:XD, :], ACT.Copy).then_inc(read["xd"], 1)

            def take_ct(f):
                wait_full(act, "ct", f, 0)
                nc.scalar.activation(ct[:, f.par, :, :],
                                     G[BANK["ct", 0]][:, 0:TB * XD].rearrange("p (a e) -> p a e", e=XD),
                                     ACT.Copy).then_inc(read["ct"], 1)

            def take_dt(f, i):
                wait_full(act, "dt", f, i)
                nc.scalar.activation(dt[:, f.par, i, :], G[BANK["dt", i]][:, :], ACT.Identity, bias=bdt[:, i:i + 1])\
                    .then_inc(read["dt"], 1)

            def softplus_e(f, q):
                if q == 0:
                    wait(act, hist_saved, f, 1, 1)
                wait_read(act, "dt", f, 2 * q + 1)
                nc.scalar.activation(t2(q), dt[:, f.par, quarter(q), :], ACT.Abs).then_inc(abs_ready, 1)
                wait(act, abs_ready, f, 4, q + 1)
                nc.scalar.activation(t2(q), t2(q), ACT.Exp, scale=-1.0).then_inc(e_ready, 1)

            def softplus_ln(f, q):
                wait(act, u_ready, f, 4, q + 1)
                if q >= 2:
                    wait(act, dt_ready, f, 4, q - 1)
                nc.scalar.activation(t3(q), t2(q), ACT.Ln).then_inc(l1_ready, 1)
                wait(act, l1_ready, f, 4, q + 1)
                nc.scalar.activation(t3(q), t3(q), ACT.Ln)
                nc.scalar.activation(t2(q), t2(q), ACT.Ln, bias=minus1[:, :]).then_inc(l23_ready, 1)

            def softplus_abs(f, q):
                wait(act, s1_ready, f, 4, q + 1)
                nc.scalar.activation(t2(q), dt[:, f.par, quarter(q), :], ACT.Abs).then_inc(abs2_ready, 1)

            def softplus_exp(f, q):
                wait(act, s_ready, f, 4, q + 1)
                nc.scalar.activation(t3(q), t3(q), ACT.Exp).then_inc(log1p_ready, 1)

            def take_z(c, i):
                if i == 0:
                    wait(act, gated, c, NB, 0)
                wait_full(act, "z", c, i)
                nc.scalar.activation(z[:, i, :], G[BANK["z", i]][:, :], ACT.Copy).then_inc(read["z"], 1)

            def silu_z(c):
                wait_read(act, "z", c, NB - 1)
                for i in range(NB):
                    nc.scalar.activation(z[:, i, :], z[:, i, :], ACT.Silu).then_inc(z_ready, 1)

            def norm_scale(p):
                wait(act, mv_ready, p, 1, 1)
                nc.scalar.activation(lnv[:, :], mv[:, :, 1], ACT.Ln, bias=epsln[:, :]).then_inc(lnv_ready, 1)
                wait(act, lnv_ready, p, 1, 1)
                nc.scalar.activation(rstd[:, :], lnv[:, :], ACT.Exp, scale=-0.5).then_inc(rstd_ready, 1)

            first = Chunk(0, 0)
            for i in range(NB):
                take_x(first, i)
            silu_x(first, range(NB))
            take_xd(first)
            take_ct(first)
            for i in range(NB):
                take_dt(first, i)
            for q in range(5):
                if q < 4:
                    softplus_e(first, q)
                    softplus_ln(first, q)
                    softplus_abs(first, q)
                if q:
                    softplus_exp(first, q - 1)
            for j in range(HB):
                decay(first, 0, j)

            def chunk(c, is_first, is_last):
                p, f = c.near(-1), c.near(1)
                for s in range(STEPS):
                    for j in range(HB):
                        if s + 1 < STEPS:
                            decay(c, s + 1, j)
                        elif not is_last:
                            decay(f, 0, j)
                        if j == 1 and not is_last:
                            if s - 1 in SP_STEP:
                                softplus_ln(f, SP_STEP[s - 1])
                        if 1 <= j <= 2 and not is_last:
                            for i in DT_AT.get(s - 1, ())[j - 1:j]:
                                take_dt(f, i)
                        if j == 2 and not is_last:
                            if s - 3 in SP_STEP:
                                softplus_exp(f, SP_STEP[s - 3])
                            if s in SP_STEP:
                                softplus_e(f, SP_STEP[s])
                        if j == 3 and s - 2 in SP_STEP and not is_last:
                            softplus_abs(f, SP_STEP[s - 2])
                    if s == CONV_STEP:
                        for i in range(HB):
                            if i < 2:
                                take_z(c, i)
                            if not is_last:
                                silu_x(f, (2 * i, 2 * i + 1))
                        if not is_last:
                            take_xd(f)
                    if not is_last:
                        if 1 <= s <= NB:
                            take_x(f, s - 1)
                        if s == CONV_STEP + 2:
                            take_ct(f)
                    if s - 1 in Z_AT:
                        take_z(c, Z_AT[s - 1])
                    if s == LN_STEP + 1 and not is_first:
                        norm_scale(p)
                    if s == Z_SILU_STEP:
                        silu_z(c)

            walk(act, chunk)
            norm_scale(Chunk(CHUNKS // 2 - 1, 1))

        @block.vector
        def _(dve):
            dve.wait_ge(a_exp, 1)
            nc.vector.tensor_scalar(aneg[:, :, :], aneg[:, :, :], -1.0, None, ALU.mult).then_inc(a_set, 1)
            nc.vector.memset(hist[:, :, :, :], 0.0).then_inc(state_zero, 1)
            nc.vector.memset(carry[:, :, :, :], 0.0).then_inc(state_zero, 1)
            dve.wait_ge(weights_in, 16 * N_WEIGHTS)
            dve.wait_ge(state_zero, 2)

            def conv(f):
                wait(dve, hist_saved, f, 1, -1)
                nc.vector.tensor_copy(xpad[:, :, 0:KC - 1], hist[:, f.par, :, :]).then_inc(hist_put, 1)
                wait_full(dve, "o", f.near(-2), TB - 1)
                wait(dve, hist_put, f, 1, 1)
                for i in range(0, NB, 2):
                    for k in range(KC - 1, -1, -1):
                        for e in (i, i + 1):
                            if k == KC - 1:
                                wait_read(dve, "x", f, e)
                                ins = nc.vector.tensor_scalar(x[:, f.par, e, :], xpad[:, e, k:k + TC], cw[:, e, k:k + 1],
                                                              cb[:, e:e + 1], ALU.mult, ALU.add)
                            else:
                                wait(dve, conv_step, f, NB * KC, i * KC + 2 * (KC - 2 - k) + (e - i) + 1)
                                ins = nc.vector.scalar_tensor_tensor(x[:, f.par, e, :], xpad[:, e, k:k + TC],
                                                                     cw[:, e, k:k + 1], x[:, f.par, e, :],
                                                                     ALU.mult, ALU.add)
                            ins.then_inc(conv_step, 1)
                nc.vector.tensor_copy(hist[:, f.par, :, :], xpad[:, :, TC:]).then_inc(hist_saved, 1)

            def softplus_u(f, q):
                wait(dve, e_ready, f, 4, q + 1)
                nc.vector.tensor_scalar(t2(q), t2(q), 1.0, ONE_UP, ALU.add, ALU.max).then_inc(u_ready, 1)

            def softplus_ratio(f, q):
                wait(dve, l23_ready, f, 4, q + 1)
                nc.vector.tensor_tensor(t3(q), t3(q), t2(q), ALU.subtract).then_inc(s1_ready, 1)

            def softplus_s(f, q):
                wait(dve, abs2_ready, f, 4, q + 1)
                nc.vector.tensor_tensor(t3(q), t3(q), t2(q), ALU.subtract).then_inc(s_ready, 1)

            def softplus_sum(f, q):
                wait(dve, log1p_ready, f, 4, q + 1)
                nc.vector.scalar_tensor_tensor(dt[:, f.par, quarter(q), :], dt[:, f.par, quarter(q), :], 0.0, t3(q),
                                               ALU.max, ALU.add).then_inc(dt_ready, 1)

            def softplus(f, s):
                if s - 2 in SP_STEP:
                    softplus_ratio(f, SP_STEP[s - 2])
                if s - 1 in SP_STEP:
                    softplus_u(f, SP_STEP[s - 1])
                if s - 3 in SP_STEP:
                    softplus_s(f, SP_STEP[s - 3])

            def make_dtx(f, q):
                wait(dve, dt_ready, f, 4, q + 1)
                if q == 0:
                    wait(dve, x_ready, f, NB, NB)
                nc.vector.tensor_tensor(dtx[:, quarter(q), :], dt[:, f.par, quarter(q), :], x[:, f.par, quarter(q), :],
                                        ALU.mult).then_inc(dtx_ready, 1)

            def scan(c, s, j):
                n, hf = s // 2, s % 2
                if j == 0:
                    wait(dve, ht_full, c, ADDS, (s - 1) * TB)
                    wait(dve, carried, c, STEPS, s - 1)
                k = s * HB + j
                i = hf * HB + j
                wait(dve, decay_ready, c, SCANS, k + 1)
                if j % 2 == 0:
                    wait(dve, dbu_ready, c, DBUS, k // 2 + 1)
                nc.vector.tensor_tensor_scan(h[:, hf, j, :], DA[k % 4][:, :], dbu[:, k // 2 % 2, j % 2, :],
                                             carry[:, c.par, n, i:i + 1], ALU.mult, ALU.add).then_inc(scanned, 1)

            def add_to_y(c, s, tb):
                n, hf = s // 2, s % 2
                q = s * TB + tb
                wait(dve, ht_full, c, ADDS, q + 1)
                dst = yt[:, tb, hf * 512:hf * 512 + 512]
                cc = ct[:, c.par, tb, DTR + NS + n:DTR + NS + n + 1]
                if n == 0:
                    ins = nc.vector.tensor_scalar(dst, HT[q % 2][:, :], cc, None, ALU.mult)
                else:
                    wait(dve, y_added, c, ADDS, q - 2 * TB + 1)
                    ins = nc.vector.scalar_tensor_tensor(dst, HT[q % 2][:, :], cc, dst, ALU.mult, ALU.add)
                ins.then_inc(y_added, 1)

            def skip(p, i):
                wait_full(dve, "y", p, i)
                nc.vector.scalar_tensor_tensor(x[:, p.par, i, :], x[:, p.par, i, :], dsk[:, i:i + 1],
                                               G[BANK["y", i]][:, :], ALU.mult, ALU.add).then_inc(read["y"], 1)

            def residual(p, tb):
                if tb == 0:
                    wait(dve, x_in, p, 16, 16)
                wait_full(dve, "o", p, tb)
                nc.vector.tensor_tensor(xres[:, tb, :], G[BANK["o", tb]][:, :], xres[:, tb, :], ALU.add)\
                    .then_inc(read["o"], 1)

            def norm_sums(p):
                for tb in range(TB):
                    wait_read(dve, "o", p, tb)
                    nc.vector.bn_stats(stats[:, tb, :], xres[:, tb, :]).then_inc(stats_ready, 1)
                wait(dve, stats_ready, p, TB, TB)
                dve.sem_inc(stats_seen, 1)
                for tb in range(TB):
                    ins = nc.vector.bn_aggr(mv[:, tb, :], stats[:, tb, :])
                ins.then_inc(mv_ready, 1)

            def norm_apply(p):
                wait(dve, rstd_ready, p, 1, 1)
                for tb in range(TB):
                    ins = nc.vector.tensor_scalar(xres[:, tb, :], xres[:, tb, :], mv[:, tb, 0:1], rstd[:, tb:tb + 1],
                                                  ALU.subtract, ALU.mult)
                ins.then_inc(x1_ready, 1)

            first = Chunk(0, 0)
            conv(first)
            for q in range(5):
                if q < 4:
                    softplus_u(first, q)
                    softplus_ratio(first, q)
                    softplus_s(first, q)
                if q:
                    softplus_sum(first, q - 1)
                    make_dtx(first, q - 1)

            def chunk(c, is_first, is_last):
                p, f = c.near(-1), c.near(1)
                for s in range(STEPS):
                    for j in range(HB):
                        scan(c, s, j)
                        if s:
                            add_to_y(c, s - 1, j)
                        elif not is_first:
                            add_to_y(p, STEPS - 1, j)
                        if j == 1 and not is_last:
                            softplus(f, s)
                    if not is_first:
                        if s == 0:
                            for i in range(NB):
                                skip(p, i)
                        if s in RESIDUAL_STEP:
                            residual(p, RESIDUAL_STEP[s])
                        if s == LN_STEP:
                            norm_sums(p)
                        if s == LN_STEP + 2:
                            norm_apply(p)
                    if not is_last:
                        if s == CONV_STEP:
                            conv(f)
                        if s - 4 in SP_STEP:
                            softplus_sum(f, SP_STEP[s - 4])
                        if s >= STEPS - 2:
                            for q in range(2 * (s % 2), 2 * (s % 2) + 2):
                                make_dtx(f, q)

            walk(dve, chunk)
            last = Chunk(CHUNKS // 2 - 1, 1)
            for tb in range(TB):
                add_to_y(last, STEPS - 1, tb)
            for i in range(NB):
                skip(last, i)
            for tb in range(TB):
                residual(last, tb)
            norm_sums(last)
            norm_apply(last)

        @block.tensor
        def _(pe):
            pe.wait_ge(ident_set, 1)

            def in_proj(kind, chunk, i, parts, room):
                if 0 in parts:
                    room(kind, chunk, i)
                    if i == 0:
                        wait(pe, xt_in[kind], chunk, 16, 16)
                    wait(pe, win_in[kind][i % 2], chunk, NB // 2 * 16, (i // 2 + 1) * 16)
                for k in parts:
                    ins = nc.tensor.matmul(G[BANK[kind, i]][:, :], win[:, i % 2, k, :], xt[:, k, :],
                                           start=(k == 0), stop=(k == KM - 1))
                if KM - 1 in parts:
                    ins.then_inc(full[kind], 1)

            def x_proj(f, parts, room):
                if 0 in parts:
                    room("xd", f, 0)
                for i in parts:
                    wait(pe, x_ready, f, NB, i + 1)
                    ins = nc.tensor.matmul(G[BANK["xd", 0]][0:XD, :], wxp[:, i, :], x[:, f.par, i, :],
                                           start=(i == 0), stop=(i == NB - 1))
                if NB - 1 in parts:
                    ins.then_inc(full["xd"], 1)

            def transpose_xd(f, room):
                wait_read(pe, "xd", f, 0)
                room("ct", f, 0)
                for tb in range(TB):
                    ins = nc.tensor.transpose(G[BANK["ct", 0]][:, tb * XD:(tb + 1) * XD], xdbl[:, tb * P:(tb + 1) * P],
                                              ident[0:XD, 0:XD])
                ins.then_inc(full["ct"], 1)

            def dt_proj(f, i, room):
                room("dt", f, i)
                nc.tensor.matmul(G[BANK["dt", i]][:, :], wdt[:, i * P:(i + 1) * P], xdbl[0:DTR, :], start=True,
                                 stop=True).then_inc(full["dt"], 1)

            def transpose_y(p, i, room):
                if i == 0:
                    wait(pe, y_added, p, ADDS, ADDS)
                room("y", p, i)
                for tb in range(TB):
                    ins = nc.tensor.transpose(G[BANK["y", i]][:, tb * P:(tb + 1) * P], yt[:, tb, i * P:(i + 1) * P],
                                              ident[:, :])
                ins.then_inc(full["y"], 1)

            def out_proj(p, tb, parts, room):
                if 0 in parts:
                    room("o", p, tb)
                for i in parts:
                    if tb == 0:
                        wait(pe, gated, p, NB, i + 1)
                    ins = nc.tensor.matmul(G[BANK["o", tb]][:, :], x[:, p.par, i, tb * P:(tb + 1) * P], wout[:, i, :],
                                           start=(i == 0), stop=(i == NB - 1))
                if NB - 1 in parts:
                    ins.then_inc(full["o"], 1)

            def transpose_h(c, s, tb):
                q = s * TB + tb
                if tb == 0:
                    wait(pe, scanned, c, SCANS, (s + 1) * HB)
                wait(pe, y_added, c, ADDS, q - 1)
                for j in range(HB):
                    ins = nc.tensor.transpose(HT[q % 2][:, j * P:(j + 1) * P], h[:, s % 2, j, tb * P:(tb + 1) * P],
                                              ident[:, :])
                ins.then_inc(ht_full, 1)

            def rooms(held):
                def room(kind, chunk, i):
                    bank = BANK[kind, i]
                    if held[bank]:
                        wait_read(pe, held[bank][0], held[bank][1], held[bank][2])
                    held[bank] = (kind, chunk, i)
                return room

            def last_z(p):
                held = [None, None]
                for i in (NB - 2, NB - 1):
                    held[BANK["z", i]] = ("z", p, i)
                return held

            first = Chunk(0, 0)
            room = prologue = rooms([None, None])
            for i in range(NB):
                in_proj("x", first, i, range(KM), room)
            pe.wait_ge(weights_in, 16 * N_WEIGHTS)
            x_proj(first, range(NB), room)
            transpose_xd(first, room)
            for i in range(NB):
                dt_proj(first, i, room)

            def chunk(c, is_first, is_last):
                p, f = c.near(-1), c.near(1)
                room = prologue if is_first else rooms(last_z(p))

                def slot(s, tb):
                    for kind, i, parts in SLOTS.get((s, tb), ()):
                        if kind == "z":
                            in_proj("z", c, i, parts, room)
                        elif kind == "o":
                            if not is_first:
                                out_proj(p, i, parts, room)
                        elif not is_last:
                            if kind == "x":
                                in_proj("x", f, i, parts, room)
                            elif kind == "xd":
                                x_proj(f, parts, room)
                            elif kind == "ct":
                                transpose_xd(f, room)
                            else:
                                dt_proj(f, i, room)

                if not is_first:
                    for i in range(NB):
                        transpose_y(p, i, room)
                for s in range(STEPS):
                    for tb in range(TB):
                        transpose_h(c, s, tb)
                        slot(s, tb)

            walk(pe, chunk)
            last = Chunk(CHUNKS // 2 - 1, 1)
            room = rooms(last_z(last))
            for i in range(NB):
                transpose_y(last, i, room)
            for tb in range(TB):
                out_proj(last, tb, range(NB), room)


def ffn_phase(nc, x1, w1, b1, w2, b2, out):
    ctx = ExitStack()
    with ctx:
        def sb(name, shape, dt=F32):
            return ctx.enter_context(nc.sbuf_tensor(name, shape, dt))

        def sem(name):
            return ctx.enter_context(nc.semaphore(name))

        w1q = sb("w1q", [P, KM, DFF], F32R)
        w2q = sb("w2q", [P, NJ, DM], F32R)
        raw = sb("raw", [P, 2, KM * DFF])
        below = sb("below", [P, DFF])
        ident = sb("ident2", [P, P])
        ones = sb("ones", [P, P])
        sums = sb("sums", [P, 2])
        thr = sb("thr", [P, 2, 2])
        b1c = sb("b1c", [P, NJ])
        b2r = sb("b2r", [P, DM])
        epsln = sb("epsln2", [P, 1])
        xr = sb("xr", [P, 2, TB, DM])
        xhi = sb("xhi", [P, KM, TC], F32R)
        xlo = sb("xlo", [P, KM, TC], F32R)
        hr = sb("hr", [P, 2, TC])
        hhi = sb("hhi", [P, 2, TC], F32R)
        hlo = sb("hlo", [P, 2, TC], F32R)
        stats = sb("stats2", [P, TB, 6])
        mv = sb("mv2", [P, TB, 2])
        lnv = sb("lnv2", [P, TB])
        rstd = sb("rstd2", [P, TB])

        XT = [ctx.enter_context(nc.psum_tensor(f"xt_ps{i}", [P, TC], F32)) for i in range(2)]
        HP = [ctx.enter_context(nc.psum_tensor(f"hidden_ps{i}", [P, TC], F32)) for i in range(2)]
        OP = [ctx.enter_context(nc.psum_tensor(f"out_ps{i}", [P, DM], F32)) for i in range(TB)]

        raw_in = sem("raw_in")
        raw2_in = sem("raw2_in")
        bias_in = sem("bias_in")
        consts_set = sem("consts_set2")
        ident_zero = sem("ident_zero2")
        ident_set = sem("ident_set2")
        sums_ready = sem("sums_ready")
        total_ready = sem("total_ready")
        thr_step = sem("thr_step")
        below_ready = sem("below_ready")
        quantised = sem("quantised")
        x_in = [sem("xr_in0"), sem("xr_in1")]
        xt_full = sem("xt_full")
        hi_ready = sem("hi_ready")
        lo_ready = sem("lo_ready")
        hp_full = sem("hp_full")
        relu_done = sem("relu_done")
        hhi_ready = sem("hhi_ready")
        hlo_ready = sem("hlo_ready")
        h_used = sem("h_used")
        res_ready = sem("res_ready")
        added = sem("added")
        stats_ready = sem("stats_ready2")
        stats_seen = sem("stats_seen2")
        mv_ready = sem("mv_ready2")
        lnv_ready = sem("lnv_ready2")
        rstd_ready = sem("rstd_ready2")
        y_ready = sem("y_ready")
        stored = [sem("stored0"), sem("stored1")]

        block = ctx.enter_context(nc.Block())
        PAIRS = CHUNKS // 2

        @block.sync
        def _(sp):
            sp.dma_start(raw[:, 0, :].rearrange("p (k f) -> p k f", k=KM), w1.rearrange("(k p) f -> p k f", p=P))\
                .then_inc(raw_in, 16)
            sp.dma_start(raw[:, 1, :].rearrange("p (j e) -> p j e", j=NJ), w2.rearrange("(j p) e -> p j e", p=P))\
                .then_inc(raw2_in, 16)
            sp.dma_start(b1c[:, :], b1).then_inc(bias_in, 16)
            sp.dma_start(b2r[:, :], b2.rearrange("(o e) -> o e", o=1).to_broadcast([P, DM])).then_inc(bias_in, 16)

            def load(first, par):
                sp.dma_start(xr[:, par, :, :], x1[bass.ds(first, TC), :].rearrange("(a p) e -> p a e", p=P))\
                    .then_inc(x_in[par], 16)

            def store(it, first, par):
                sp.wait_ge(y_ready, it + 1)
                sp.dma_start(out[bass.ds(first, TC), :].rearrange("(a p) e -> p a e", p=P), xr[:, par, :, :])\
                    .then_inc(stored[par], 16)

            load(0, 0)
            load(TC, 1)
            with sp.Fori(0, PAIRS - 1) as i:
                firsts = [sp.snap(i * (2 * TC) + par * TC) for par in range(4)]
                for par in range(2):
                    store(2 * i + par, firsts[par], par)
                    sp.wait_ge(stored[par], i * 16 + 16)
                    load(firsts[par + 2], par)
            for par in range(2):
                store(CHUNKS - 2 + par, (CHUNKS - 2 + par) * TC, par)
            for par in range(2):
                sp.wait_ge(stored[par], PAIRS * 16)

        @block.gpsimd
        def _(pool):
            nc.gpsimd.memset(epsln[:, :], EPS_LN).then_inc(consts_set, 1)
            nc.gpsimd.memset(ones[:, :], 1.0).then_inc(consts_set, 1)
            nc.gpsimd.memset(ident[:, :], 0.0).then_inc(ident_zero, 1)
            pool.wait_ge(ident_zero, 1)
            nc.gpsimd.affine_select(out=ident[:, :], in_=ident[:, :], compare_op=ALU.not_equal, fill=1.0,
                                    base=0, pattern=[[-1, P]], channel_multiplier=1).then_inc(ident_set, 1)
            pool.sem_inc(added, TB)

        def chunk_order(eng, body):
            with eng.Fori(0, PAIRS - 1) as i:
                for par in range(2):
                    body(i, 2 * i + par, par, False)
            body(PAIRS - 1, CHUNKS - 2, 0, False)
            body(PAIRS - 1, CHUNKS - 1, 1, True)

        @block.scalar
        def _(act):
            act.wait_ge(bias_in, 32)
            act.wait_ge(consts_set, 2)

            def split_hi(it):
                for k in range(KM):
                    act.wait_ge(xt_full, it * KM + k + 1)
                    nc.scalar.activation(xhi[:, k, :], XT[k % 2][:, :], ACT.Copy).then_inc(hi_ready, 1)

            split_hi(0)

            def chunk(i, it, par, last):
                for j in range(NJ):
                    act.wait_ge(hp_full, it * NJ + j + 1)
                    if j >= 2:
                        act.wait_ge(hlo_ready, it * NJ + j - 1)
                    nc.scalar.activation(hr[:, j % 2, :], HP[j % 2][:, :], ACT.Relu, bias=b1c[:, j:j + 1])\
                        .then_inc(relu_done, 1)
                if not last:
                    split_hi(it + 1)
                act.wait_ge(mv_ready, it + 1)
                nc.scalar.activation(lnv[:, :], mv[:, :, 1], ACT.Ln, bias=epsln[:, :]).then_inc(lnv_ready, 1)
                act.wait_ge(lnv_ready, it + 1)
                nc.scalar.activation(rstd[:, :], lnv[:, :], ACT.Exp, scale=-0.5).then_inc(rstd_ready, 1)

            chunk_order(act, chunk)

        @block.vector
        def _(dve):
            dve.wait_ge(raw_in, 16)
            nc.vector.tensor_reduce(sums[:, 0:1], raw[:, 0, :], AX.X, ALU.add, apply_absolute_value=True)\
                .then_inc(sums_ready, 1)
            dve.wait_ge(raw2_in, 16)
            nc.vector.tensor_reduce(sums[:, 1:2], raw[:, 1, :], AX.X, ALU.add, apply_absolute_value=True)\
                .then_inc(sums_ready, 1)
            dve.wait_ge(total_ready, 1)
            nc.vector.tensor_scalar(thr[:, :, 0], XT[0][:, 0:2], 0.5 / (DFF * DM), 0.5 * EPS_Q, ALU.mult, ALU.add)\
                .then_inc(thr_step, 1)
            dve.wait_ge(thr_step, 1)
            nc.vector.tensor_scalar(thr[:, :, 1], thr[:, :, 0], -1.0, None, ALU.mult).then_inc(thr_step, 1)
            dve.wait_ge(thr_step, 2)
            for w in range(2):
                wq = (w1q if w == 0 else w2q)[:, :, :].rearrange("p a b -> p (a b)")
                for c in range(KM):
                    part = slice(c * DFF, (c + 1) * DFF)
                    n = w * KM + c
                    if n:
                        dve.wait_ge(quantised, n)
                    nc.vector.tensor_scalar(below[:, :], raw[:, w, part], thr[:, w, 1:2], None, ALU.is_lt)\
                        .then_inc(below_ready, 1)
                    dve.wait_ge(below_ready, n + 1)
                    nc.vector.scalar_tensor_tensor(wq[:, part], raw[:, w, part], thr[:, w, 0:1], below[:, :],
                                                   ALU.is_gt, ALU.subtract).then_inc(quantised, 1)

            def split_lo(it):
                for k in range(KM):
                    dve.wait_ge(hi_ready, it * KM + k + 1)
                    nc.vector.tensor_tensor(xlo[:, k, :], XT[k % 2][:, :], xhi[:, k, :].bitcast(F32), ALU.subtract)\
                        .then_inc(lo_ready, 1)

            split_lo(0)

            def chunk(i, it, par, last):
                for j in range(NJ):
                    dve.wait_ge(relu_done, it * NJ + j + 1)
                    if j >= 2:
                        dve.wait_ge(h_used, it * NJ + j - 1)
                    nc.vector.tensor_copy(hhi[:, j % 2, :], hr[:, j % 2, :]).then_inc(hhi_ready, 1)
                    dve.wait_ge(hhi_ready, it * NJ + j + 1)
                    nc.vector.tensor_tensor(hlo[:, j % 2, :], hr[:, j % 2, :], hhi[:, j % 2, :].bitcast(F32),
                                            ALU.subtract).then_inc(hlo_ready, 1)
                    if j >= 8 and j < 8 + TB:
                        tb = j - 8
                        nc.vector.tensor_tensor(xr[:, par, tb, :], xr[:, par, tb, :], b2r[:, :], ALU.add)\
                            .then_inc(res_ready, 1)
                if not last:
                    split_lo(it + 1)
                dve.wait_ge(h_used, it * NJ + NJ)
                dve.wait_ge(res_ready, it * TB + TB)
                for tb in range(TB):
                    nc.vector.tensor_tensor(xr[:, par, tb, :], OP[tb][:, :], xr[:, par, tb, :], ALU.add).then_inc(added, 1)
                for tb in range(TB):
                    dve.wait_ge(added, it * TB + TB + tb + 1)
                    nc.vector.bn_stats(stats[:, tb, :], xr[:, par, tb, :]).then_inc(stats_ready, 1)
                dve.wait_ge(stats_ready, it * TB + TB)
                dve.sem_inc(stats_seen, 1)
                for tb in range(TB):
                    ins = nc.vector.bn_aggr(mv[:, tb, :], stats[:, tb, :])
                ins.then_inc(mv_ready, 1)
                dve.wait_ge(rstd_ready, it + 1)
                for tb in range(TB):
                    ins = nc.vector.tensor_scalar(xr[:, par, tb, :], xr[:, par, tb, :], mv[:, tb, 0:1],
                                                  rstd[:, tb:tb + 1], ALU.subtract, ALU.mult)
                ins.then_inc(y_ready, 1)

            chunk_order(dve, chunk)

        @block.tensor
        def _(pe):
            pe.wait_ge(consts_set, 2)
            pe.wait_ge(sums_ready, 2)
            nc.tensor.matmul(XT[0][:, 0:2], ones[:, :], sums[:, :], start=True, stop=True).then_inc(total_ready, 1)
            pe.wait_ge(ident_set, 1)
            pe.wait_ge(quantised, 2 * KM)

            def transposes(it, par, i, blocks):
                pe.wait_ge(x_in[par], i * 16 + 16)
                for k in blocks:
                    if k >= 2:
                        pe.wait_ge(lo_ready, it * KM + k - 1)
                    for tb in range(TB):
                        ins = nc.tensor.transpose(XT[k % 2][:, tb * P:(tb + 1) * P],
                                                  xr[:, par, tb, k * P:(k + 1) * P], ident[:, :])
                    ins.then_inc(xt_full, 1)

            transposes(0, 0, 0, range(KM))

            def chunk(i, it, par, last):
                def up(j):
                    if j >= 2:
                        pe.wait_ge(relu_done, it * NJ + j - 1)
                    for k in range(KM):
                        for part in (xhi, xlo):
                            ins = nc.tensor.matmul(HP[j % 2][:, :], w1q[:, k, j * P:(j + 1) * P], part[:, k, :],
                                                   start=(k == 0 and part is xhi), stop=(k == KM - 1 and part is xlo))
                    ins.then_inc(hp_full, 1)

                def down(j):
                    pe.wait_ge(hlo_ready, it * NJ + j + 1)
                    for tb in range(TB):
                        if j == 0:
                            pe.wait_ge(added, it * TB + tb + 1)
                        for part in (hhi, hlo):
                            ins = nc.tensor.matmul(OP[tb][:, :], part[:, j % 2, tb * P:(tb + 1) * P], w2q[:, j, :],
                                                   start=(j == 0 and part is hhi), stop=(j == NJ - 1 and part is hlo))
                    ins.then_inc(h_used, 1)

                pe.wait_ge(lo_ready, it * KM + KM)
                up(0)
                for j in range(NJ):
                    if j + 1 < NJ:
                        up(j + 1)
                    if j == NJ - 2 and not last:
                        transposes(it + 1, 1 - par, i + par, range(2))
                    down(j)
                    if j == NJ - 2 and not last:
                        transposes(it + 1, 1 - par, i + par, range(2, KM))

            chunk_order(pe, chunk)


def build(nc, x_tm, x_cm, w_in, conv_w, conv_b, w_xp, w_dt, b_dt, a_log, d_skip, w_out, w1, b1, w2, b2, out):
    nc.disable_value_cache = True
    b_rows = nc.dram_tensor("b_rows", [2, NS, TC], F32, kind="Internal").ap()
    x1 = nc.dram_tensor("x1", [BATCH * SEQ, DM], F32, kind="Internal").ap()
    mixer_phase(nc, x_tm, x_cm, w_in, conv_w, conv_b, w_xp, w_dt, b_dt, a_log, d_skip, w_out, b_rows, x1)
    ffn_phase(nc, x1, w1, b1, w2, b2, out)


def kernel(L0_attn_hidden_states, L0_attn_in_proj_w, L0_attn_conv_w, L0_attn_conv_b, L0_attn_x_proj_w,
           L0_attn_dt_proj_w, L0_attn_dt_proj_b, L0_attn_A_log, L0_attn_D, L0_attn_out_proj_w,
           L0_ffn_W1, L0_ffn_b1, L0_ffn_W2, L0_ffn_b2):
    import numpy as np
    import concourse.bacc as bacc
    from concourse.bass_utils import run_bass_kernel_spmd

    tokens = np.asarray(L0_attn_hidden_states).reshape(BATCH * SEQ, DM)
    arrays = {
        "x_tm": tokens,
        "x_cm": tokens.T,
        "w_in": np.asarray(L0_attn_in_proj_w).reshape(2 * NB, P, KM, P).transpose(0, 3, 2, 1),
        "conv_w": np.asarray(L0_attn_conv_w).reshape(NB, P, KC).transpose(1, 0, 2),
        "conv_b": np.asarray(L0_attn_conv_b).reshape(NB, P).T,
        "w_xp": np.asarray(L0_attn_x_proj_w).T,
        "w_dt": np.asarray(L0_attn_dt_proj_w).T,
        "b_dt": np.asarray(L0_attn_dt_proj_b).reshape(NB, P).T,
        "a_log": np.asarray(L0_attn_A_log).reshape(NB, P, NS).transpose(1, 0, 2),
        "d_skip": np.asarray(L0_attn_D).reshape(NB, P).T,
        "w_out": np.asarray(L0_attn_out_proj_w).T,
        "w1": np.asarray(L0_ffn_W1).T,
        "b1": np.asarray(L0_ffn_b1).reshape(NJ, P).T,
        "w2": np.asarray(L0_ffn_W2).T,
        "b2": L0_ffn_b2,
    }
    arrays = {name: np.ascontiguousarray(a) for name, a in arrays.items()}
    nc = bacc.Bacc("TRN2", target_bir_lowering=False, num_devices=1)
    args = [nc.dram_tensor(name, a.shape, F32, kind="ExternalInput").ap() for name, a in arrays.items()]
    out = nc.dram_tensor("out", [BATCH * SEQ, DM], F32, kind="ExternalOutput").ap()
    build(nc, *args, out)
    r = run_bass_kernel_spmd(nc, [arrays], core_ids=[0])
    return np.asarray(r.results[0]["out"]).reshape(BATCH, SEQ, DM)
```
